# Optimizing a Trainium2 kernel written in Bass

```python
import numpy as np
import jax
import jax.numpy as jnp

def _softmax(x, axis=-1):
    return jax.nn.softmax(x, axis=axis)

def _gelu(x):
    return jax.nn.gelu(x, approximate=True)

def _silu(x):
    return jax.nn.silu(x)

def _sigmoid(x):
    return jax.nn.sigmoid(x)

def _layernorm(x, axis=-1, eps=1e-05):
    m = jnp.mean(x, axis=axis, keepdims=True)
    v = jnp.var(x, axis=axis, keepdims=True)
    return (x - m) / jnp.sqrt(v + eps)

def _scatter_add(tgt, idx, src, axis=0):
    return tgt.at[idx].add(src)

def _segment_sum(src, seg, n):
    return jax.ops.segment_sum(src, seg, n)
kernel_name = 'mk_rec_standalone_d1_rec_r8_16b425'

def setup_inputs(seed: int=0):
    np.random.seed(seed)
    _w = jnp.asarray

    def _rec_inputs():
        import jax
        import jax.numpy as jnp
        _rk = jax.random.key(seed)
        r_input = jax.random.randint(jax.random.fold_in(_rk, 1), (512, 200), 78, 199964, jnp.int32)
        return r_input
    r_input = _rec_inputs()

    def _L0_rec_setup():
        import jax, jax.numpy as jnp
        import numpy as np
        NTOKEN = 25000
        NINP = 64

        def gcn_conv(x, W, b, row, col, num_nodes):
            h = x @ W
            loop = jnp.arange(num_nodes, dtype=row.dtype)
            row_sl = jnp.concatenate([row, loop])
            col_sl = jnp.concatenate([col, loop])
            deg = jax.ops.segment_sum(jnp.ones_like(col_sl, dtype=h.dtype), col_sl, num_segments=num_nodes)
            dinv = jax.lax.rsqrt(jnp.maximum(deg, 1.0))
            norm = dinv[row_sl] * dinv[col_sl]
            msg = h[row_sl] * norm[:, None]
            out = jax.ops.segment_sum(msg, col_sl, num_segments=num_nodes)
            return out + b
        key = jax.random.key(seed)
        k1, k2, k3, k4, k5, k6, k7 = jax.random.split(key, 7)
        B, L, E = (64, 200, 250000)
        inp = jax.random.randint(k1, (B, L), 0, NTOKEN, dtype=jnp.int64 if jax.config.jax_enable_x64 else jnp.int32)
        input_timestamp = jax.random.randint(k2, (B, L), 0, 37500)
        input_id = jax.random.randint(k3, (B,), 0, NTOKEN)
        edge_index = jax.random.randint(k4, (2, E), 0, NTOKEN)
        emb = jax.random.normal(k5, (NTOKEN, NINP), dtype=jnp.float32) * np.sqrt(2.0 / (NTOKEN + NINP))
        emb = emb.at[0].set(0.0)
        W1 = jax.random.normal(k6, (NINP, 2 * NINP), dtype=jnp.float32) * np.sqrt(2.0 / (3 * NINP))
        b1 = jnp.zeros((2 * NINP,), dtype=jnp.float32)
        W2 = jax.random.normal(k7, (2 * NINP, NINP), dtype=jnp.float32) * np.sqrt(2.0 / (3 * NINP))
        b2 = jnp.zeros((NINP,), dtype=jnp.float32)
        return {'input': inp, 'input_timestamp': input_timestamp, 'input_id': input_id, 'edge_index': edge_index, 'emb': emb, 'W1': W1, 'b1': b1, 'W2': W2, 'b2': b2}
    _L0_rec_all = _L0_rec_setup()
    _L0_rec_in = {k: v for k, v in _L0_rec_all.items() if k in ('input_timestamp', 'input_id', 'edge_index', 'emb', 'W1', 'b1', 'W2', 'b2')}
    del _L0_rec_all
    return {'r_input': r_input, 'L0_rec_input_timestamp': _L0_rec_in['input_timestamp'], 'L0_rec_input_id': _L0_rec_in['input_id'], 'L0_rec_edge_index': _L0_rec_in['edge_index'], 'L0_rec_emb': _L0_rec_in['emb'], 'L0_rec_W1': _L0_rec_in['W1'], 'L0_rec_b1': _L0_rec_in['b1'], 'L0_rec_W2': _L0_rec_in['W2'], 'L0_rec_b2': _L0_rec_in['b2']}

def reference(r_input, L0_rec_input_timestamp, L0_rec_input_id, L0_rec_edge_index, L0_rec_emb, L0_rec_W1, L0_rec_b1, L0_rec_W2, L0_rec_b2):
    import jax
    import jax.numpy as jnp

    def _L0_rec_ref(input, input_timestamp, input_id, edge_index, emb, W1, b1, W2, b2):
        import jax, jax.numpy as jnp
        import numpy as np
        NTOKEN = 25000
        NINP = 64

        def gcn_conv(x, W, b, row, col, num_nodes):
            h = x @ W
            loop = jnp.arange(num_nodes, dtype=row.dtype)
            row_sl = jnp.concatenate([row, loop])
            col_sl = jnp.concatenate([col, loop])
            deg = jax.ops.segment_sum(jnp.ones_like(col_sl, dtype=h.dtype), col_sl, num_segments=num_nodes)
            dinv = jax.lax.rsqrt(jnp.maximum(deg, 1.0))
            norm = dinv[row_sl] * dinv[col_sl]
            msg = h[row_sl] * norm[:, None]
            out = jax.ops.segment_sum(msg, col_sl, num_segments=num_nodes)
            return out + b
        row, col = (edge_index[0], edge_index[1])
        h1 = gcn_conv(emb, W1, b1, row, col, NTOKEN)
        lookup = gcn_conv(h1, W2, b2, row, col, NTOKEN)
        return lookup[input]
    y = _L0_rec_ref(r_input, L0_rec_input_timestamp, L0_rec_input_id, L0_rec_edge_index, L0_rec_emb, L0_rec_W1, L0_rec_b1, L0_rec_W2, L0_rec_b2)
    return y

_drawn_inputs = setup_inputs


def setup_inputs(seed=0):
    import zlib

    import numpy as np

    out = dict(_drawn_inputs(seed))
    spreads = {'L0_rec_b1': (0.0, 0.1), 'L0_rec_b2': (0.0, 0.1)}
    factors = {'L0_rec_emb': 8.0, 'L0_rec_W1': 8.0}
    for name, (base, spread) in spreads.items():
        noise = np.random.default_rng([zlib.crc32(name.encode()), seed]).standard_normal(out[name].shape)
        drawn = base * np.exp(spread * noise) if base else spread * noise
        out[name] = jnp.asarray(drawn.astype(out[name].dtype))
    for name, factor in factors.items():
        out[name] = (out[name] * factor).astype(out[name].dtype)
    return out
```

```python
from contextlib import ExitStack

import concourse.bass as bass
from concourse import mybir

F32 = mybir.dt.float32
BF16 = mybir.dt.bfloat16
F16 = mybir.dt.float16
I32 = mybir.dt.int32
ALU = mybir.AluOpType
ACT = mybir.ActivationFunctionType
AX = mybir.AxisListType

P = 128
NODES, FEAT, HID, EDGES = 25000, 64, 128, 250000
LOOKUPS = 512 * 200
NT = -(-NODES // P)
BT = 4
NB = NT // BT
BN = BT * P
EP = 125
EC = EDGES // EP
CHUNKS = 5
W8 = 8
CB = EC // CHUNKS // W8
CT = -(-((EC // CHUNKS * EP + NB * (P - 1)) // P) // W8) * W8
TB = CT // W8
TAIL = TB - CB
SLOTS = NB * W8
CODE = 4096
HALF = CODE // 2
PIECES, PT = 14, NT // 14
OUT_TILES = LOOKUPS // P
OUT_ITERS = OUT_TILES // (2 * W8)
CREDIT = 8
RING = 4
NOWHERE = 600.0

assert NT % BT == 0 and CT <= 512 and CB * W8 * CHUNKS == EC and TAIL > 0
assert PIECES * PT == NT and OUT_ITERS * 2 * W8 == OUT_TILES
assert P * NT * BN < CODE * CODE


def build(nc, r_input, edge_index, embT, W1T, b1, W2, b2, out):
    with ExitStack() as ctx:
        def sb(name, shape, dt):
            return ctx.enter_context(nc.sbuf_tensor(name, shape, dt))

        def sem(name):
            return ctx.enter_context(nc.semaphore(name))

        table = [nc.dram_tensor(f"table{r}", [P * NT, 3 * FEAT], BF16).ap() for r in range(2)]
        lookup = nc.dram_tensor("lookup", [P * NT, FEAT], F32).ap()
        blocks_dram = nc.dram_tensor("blocks_dram", [CHUNKS, P * BT], I32).ap()

        acc = sb("acc", [P, NT, FEAT], F32)
        edge_hi = sb("edge_hi", [P, EC], F16)
        edge_lo = sb("edge_lo", [P, EC], F16)
        edge_blk = sb("edge_blk", [P, EC], F16)
        digit = [sb(f"digit{k}", [P, EC], F32) for k in range(2)]
        digit_i = [d[:, :].bitcast(I32) for d in digit]
        scratch = sb("scratch", [P, 3 * EC], I32)
        rows, cols, bits = (scratch[:, k * EC:(k + 1) * EC] for k in range(3))
        SPN = PT * FEAT
        split = scratch[:, 0:2 * 3 * SPN // 2].bitcast(BF16).rearrange(
            "p (b t c f) -> p b t c f", b=2, t=PT, c=3)
        rest = scratch[:, 3 * SPN:3 * SPN + 2 * SPN].bitcast(F32).rearrange(
            "p (b t f) -> p b t f", b=2, t=PT)
        ramp8 = sb("ramp8", [P, 256, W8], F16)
        ramp = sb("ramp", [P, BN], F16)
        zeros_f = sb("zeros_f", [P, 512], F32)
        zeros = zeros_f[:, 0:256].bitcast(F16)
        ones = sb("ones", [P, P], F16)
        before = sb("before", [P, P], F16)
        not_before = sb("not_before", [P, P], F16)
        hi_onehot = sb("hi_onehot", [P, 2, NT, W8], F16)
        lo_onehot = sb("lo_onehot", [P, 2, P, W8], F16)
        late = sb("late", [P, RING * CT + 2 * W8 * P + RING * BN + W8 * 3 * FEAT], F16)
        emb_sb = late[0:FEAT, 0:2 * 2 * PT * P].bitcast(F32).rearrange("p (b n) -> p b n", b=2)
        w1_sb = sb("w1_sb", [HID, FEAT], F32)
        w2_sb = sb("w2_sb", [HID, FEAT], F32)
        b1_sb = sb("b1_sb", [HID, 1], F32)
        b1_rep = sb("b1_rep", [HID, P], F32)
        b2_rep = sb("b2_rep", [P, FEAT], F32)
        w12 = sb("w12", [FEAT, FEAT], F32)
        c_rep = sb("c_rep", [P, FEAT], F32)
        deg = sb("deg", [P, NT], F32)
        dinv = sb("dinv", [P, NT], F32)
        dtmp = sb("dtmp", [P, NT], F32)
        counts = sb("counts", [P, CHUNKS * SLOTS], F32)
        seed = sb("seed", [P, CHUNKS, SLOTS], F32)
        tot = sb("tot", [P, CHUNKS, NB], F32)
        tot_i = sb("tot_i", [P, CHUNKS, NB], I32)
        endt = sb("endt", [P, CHUNKS, NB], F32)
        tile_no_i = sb("tile_no_i", [P, BT], I32)
        tile_no = sb("tile_no", [P, BT], F32)
        ended = scratch[:, 5 * SPN:5 * SPN + CHUNKS * BT * NB].bitcast(F32).rearrange(
            "p (c k n) -> p c k n", c=CHUNKS, k=BT)
        blk_f = sb("blk_f", [P, CHUNKS * BT], F32)
        blk_i = sb("blk_i", [P, CHUNKS * BT], I32)
        blocks = sb("blocks", [1, CHUNKS * CT], I32)
        blk_onehot = sb("blk_onehot", [P, NB, W8], F16)
        picked = sb("picked", [P, NB, W8], F32)
        place_i = sb("place_i", [P, 3, W8], I32)
        prt16 = sb("prt16", [P, W8], F16)
        tcol = sb("tcol", [P, W8], F32)
        prt_onehot = sb("prt_onehot", [P, P, W8], F16)
        at = [0, RING * CT, RING * CT + 2 * W8 * P, RING * CT + 2 * W8 * P + RING * BN]
        tcol_onehot = late[:, at[0]:at[1]].rearrange("p (r t) -> p r t", r=RING)
        piece = late[:, at[1]:at[2]].rearrange("p (k j m) -> p k j m", k=2, j=W8)
        dec = [sb(f"dec{k}", [P, CT], F32) for k in range(2)]
        dec_i = [sb(f"dec_i{k}", [P, CT], I32) for k in range(2)]
        source = sb("source", [P, CHUNKS * CT], I32)
        target = sb("target", [P, CHUNKS * CT], F32)
        source8 = sb("source8", [P, W8], I32)
        target8 = sb("target8", [P, W8], F32)
        target_onehot = late[:, at[2]:at[3]].rearrange("p (r n) -> p r n", r=RING)
        gath = late[:, at[3]:].bitcast(BF16).rearrange("p (k f) -> p k f", k=W8)
        ramp8_i = source[:, 0:256 * W8].rearrange("p (w j) -> p w j", j=W8)
        ramp_i = target[:, 0:BN].bitcast(I32)
        ask_i = sb("ask_i", [P, OUT_TILES], I32)
        ask_t = [late[:, 2 * k * OUT_TILES:2 * (k + 1) * OUT_TILES].bitcast(I32) for k in range(2)]
        ask_f = late[:, 4 * OUT_TILES:6 * OUT_TILES].bitcast(F32)
        ask8 = sb("ask8", [P, 2, W8], I32)
        out_rows = sb("out_rows", [P, 2, W8, FEAT], F32)

        ps = ctx.enter_context(nc.psum_tensor("ps", [P, 8, 512], F32))
        rank_ps = ps[:, 0, 0:SLOTS]
        place_ps = [ps[:, 1 + k, 0:CT] for k in range(2)]
        tile_ps = [ps[:, 3 + k, 0:BT * FEAT] for k in range(RING)]
        deg_ps = ps[:, 6, 0:NT]
        count_ps = ps[:, 7, 0:SLOTS]
        EB = PT // 2
        w_ps = ps[:, 4, :]

        cols_loaded = sem("cols_loaded")
        rows_loaded = sem("rows_loaded")
        weights_loaded = sem("weights_loaded")
        ask_loaded = sem("ask_loaded")
        emb_loaded = [sem(f"emb_loaded{k}") for k in range(2)]
        ints_made = sem("ints_made")
        triangles_made = sem("triangles_made")
        ramps_cast = sem("ramps_cast")
        b1_spread = sem("b1_spread")
        w12_done = sem("w12_done")
        w12_copied = sem("w12_copied")
        emb_multiplied = sem("emb_multiplied")
        emb_copied = sem("emb_copied")
        edge_step = sem("edge_step")
        edge_cast = sem("edge_cast")
        hist_onehots = sem("hist_onehots")
        hist_added = sem("hist_added")
        chunk_counted = sem("chunk_counted")
        counts_copied = sem("counts_copied")
        deg_copied = sem("deg_copied")
        deg_step = sem("deg_step")
        root_taken = sem("root_taken")
        base_step = sem("base_step")
        blocks_stored = sem("blocks_stored")
        blocks_loaded = sem("blocks_loaded")
        rank_zeroed = sem("rank_zeroed")
        rank_seeded = sem("rank_seeded")
        blk_onehots = sem("blk_onehots")
        rank_summed = sem("rank_summed")
        rank_advanced = sem("rank_advanced")
        rank_step = sem("rank_step")
        pieces_ready = sem("pieces_ready")
        tcol_onehots = sem("tcol_onehots")
        columns_placed = sem("columns_placed")
        decode_step = sem("decode_step")
        sources_staged = sem("sources_staged")
        targets_staged = sem("targets_staged")
        target_onehots = sem("target_onehots")
        gathered = [sem(f"gathered{k}") for k in range(W8)]
        slots_taken = sem("slots_taken")
        tiles_multiplied = sem("tiles_multiplied")
        tiles_added = sem("tiles_added")
        scale_step = sem("scale_step")
        scaled = sem("scaled")
        part_hi = sem("part_hi")
        rest_hi = sem("rest_hi")
        part_mid = sem("part_mid")
        rest_mid = sem("rest_mid")
        part_lo = sem("part_lo")
        table_written = [[sem(f"table_written{r}_{b}") for b in range(2)] for r in range(2)]
        ask_step = sem("ask_step")
        lookup_scaled = sem("lookup_scaled")
        lookup_written = sem("lookup_written")
        asks_staged = [sem(f"asks_staged{h}") for h in range(2)]
        rows_fetched = [sem(f"rows_fetched{h}") for h in range(2)]
        out_written = [sem(f"out_written{h}") for h in range(2)]

        BATCHES = CHUNKS * TB
        RANK = 7
        DEC = 9
        SCALE = (0, 2)
        PAIRS = PIECES // 2

        table_v = [t.rearrange("(p i) f -> p i f", p=P) for t in table]
        lookup_v = lookup.rearrange("(p i) f -> p i f", p=P)
        QT = NT // 4

        def piece_of(i, b):
            return acc[:, bass.ds((i * 2 + b) * PT, PT), :]

        block = ctx.enter_context(nc.Block())

        @block.sync
        def _(sp):
            ei = edge_index.rearrange("a (p c) -> a p c", p=EP)
            sp.dma_start(cols[0:EP, :], ei[1]).then_inc(cols_loaded, 16)
            sp.dma_start(w1_sb[:, :], W1T).then_inc(weights_loaded, 16)
            sp.dma_start(w2_sb[:, :], W2).then_inc(weights_loaded, 16)
            sp.dma_start(b1_sb[:, :], b1.rearrange("(p a) -> p a", a=1)).then_inc(weights_loaded, 16)
            sp.dma_start(b2_rep[:, :], b2.rearrange("(a f) -> a f", a=1).broadcast_to([P, FEAT])).then_inc(weights_loaded, 16)
            for b in range(2):
                sp.dma_start(emb_sb[:, b, :], embT[:, b * PT * P:(b + 1) * PT * P]).then_inc(emb_loaded[b], 16)
            sp.dma_start(rows[0:EP, :], ei[0]).then_inc(rows_loaded, 16)
            sp.dma_start(ask_i[:, :], r_input.rearrange("(p t) -> p t", p=P)).then_inc(ask_loaded, 16)
            with sp.Fori(1, PAIRS) as i:
                for b in range(2):
                    sp.wait_ge(emb_multiplied, i * 2 + (b - 1))
                    sp.dma_start(emb_sb[:, b, :], embT[:, bass.ds((i * 2 + b) * (PT * P), PT * P)]).then_inc(emb_loaded[b], 16)
            def write_table(r):
                with sp.Fori(0, PAIRS) as i:
                    for b in range(2):
                        sp.wait_ge(part_lo, i * 2 + (r * PIECES + b + 1))
                        sp.dma_start(table_v[r][:, bass.ds((i * 2 + b) * PT, PT), :],
                                     split[:, b, :, :, :].rearrange("p t c f -> p t (c f)")).then_inc(table_written[r][b], 16)

            write_table(0)
            sp.wait_ge(base_step, BASE_STEPS)
            sp.dma_start(blocks_dram.rearrange("c (p k) -> p c k", p=P),
                         blk_i[:, :].rearrange("p (c k) -> p c k", c=CHUNKS)).then_inc(blocks_stored, 16)
            sp.wait_ge(blocks_stored, 16)
            sp.dma_start(blocks[0:1, :].rearrange("a (c t) -> a c t", c=CHUNKS),
                         blocks_dram[:, 0:CT].rearrange("(a c) t -> a c t", a=1)).then_inc(blocks_loaded, 16)
            write_table(1)
            for q in range(4):
                sp.wait_ge(lookup_scaled, 2 * (q + 1))
                sp.dma_start(lookup_v[:, q * QT:(q + 1) * QT, :], acc[:, q * QT:(q + 1) * QT, :]).then_inc(lookup_written, 16)
            out_v = out.rearrange("(p t) f -> p t f", p=P)
            with sp.Fori(0, OUT_ITERS) as i:
                for h in range(2):
                    sp.wait_ge(rows_fetched[h], i * (16 * W8) + 16 * W8)
                    sp.dma_start(out_v[:, bass.ds(i * (2 * W8) + h * W8, W8), :], out_rows[:, h, :, :]).then_inc(out_written[h], 16)
            for h in range(2):
                sp.wait_ge(out_written[h], 16 * OUT_ITERS)

        @block.gpsimd
        def _(pool):
            pool.iota(ramp8_i[:, :, :], pattern=[[1, 256], [0, W8]], base=0, channel_multiplier=0).then_inc(ints_made, 1)
            pool.memset(zeros_f[:, :], 0.0).then_inc(ints_made, 1)
            pool.memset(ones[:, :], 1.0).then_inc(ints_made, 1)
            pool.iota(ramp_i[:, :], pattern=[[1, BN]], base=0, channel_multiplier=0).then_inc(ints_made, 1)
            pool.iota(tile_no_i[:, :], pattern=[[1, BT]], base=0, channel_multiplier=BT).then_inc(ints_made, 1)
            pool.wait_ge(ints_made, 5)
            pool.affine_select(out=before[:, :], in_=ones[:, :], compare_op=ALU.is_gt, fill=0.0,
                               base=0, pattern=[[1, P]], channel_multiplier=-1).then_inc(triangles_made, 1)
            pool.affine_select(out=not_before[:, :], in_=ones[:, :], compare_op=ALU.is_ge, fill=0.0,
                               base=0, pattern=[[-1, P]], channel_multiplier=1).then_inc(triangles_made, 1)
            for r in range(2):
                with pool.Fori(0, PAIRS) as i:
                    for b in range(2):
                        pool.wait_ge(part_hi, i * 2 + (r * PIECES + b + 1))
                        pool.tensor_tensor(rest[:, b, :, :], piece_of(i, b), split[:, b, :, 0, :],
                                           ALU.subtract).then_inc(rest_hi, 1)
                pool.wait_ge(table_written[r][0], 16 * PAIRS)
                pool.wait_ge(table_written[r][1], 16 * PAIRS)
                with pool.Fori(0, BATCHES) as g:
                    for k in range(W8):
                        if k % 4 == 0:
                            pool.wait_ge(sources_staged, g * 2 + (2 * r * BATCHES + 1 + k // 4))
                        pool.wait_ge(tiles_multiplied, g * W8 + (r * BATCHES * W8 + k + 1))
                        pool.sem_inc(slots_taken, 1)
                        pool.indirect_dma_start(
                            out=gath[:, k, :], out_offset=None, in_=table[r],
                            in_offset=bass.IndirectOffsetOnAxis(ap=source8[:, k:k + 1], axis=0)).then_inc(gathered[k], 16)
            pool.wait_ge(lookup_written, 16 * 4)
            with pool.Fori(0, OUT_ITERS) as i:
                for h in range(2):
                    pool.wait_ge(asks_staged[h], i + 1)
                    pool.wait_ge(out_written[h], i * 16)
                    pool.sem_inc(slots_taken, 1)
                    for k in range(W8):
                        pool.indirect_dma_start(
                            out=out_rows[:, h, k, :], out_offset=None, in_=lookup,
                            in_offset=bass.IndirectOffsetOnAxis(ap=ask8[:, h, k:k + 1], axis=0)).then_inc(rows_fetched[h], 16)

        @block.scalar
        def _(act):
            act.wait_ge(ints_made, 5)
            act.copy(ramp8[:, :, :], ramp8_i[:, :, :]).then_inc(ramps_cast, 1)
            act.wait_ge(edge_step, 1)
            act.copy(edge_hi[0:EP, :], bits[0:EP, :]).then_inc(edge_cast, 1)
            act.wait_ge(edge_step, 2)
            act.copy(edge_lo[0:EP, :], digit_i[0][0:EP, :]).then_inc(edge_cast, 1)
            act.wait_ge(weights_loaded, 16 * 4)
            act.activation(b1_rep[:, :], ones[:, :], ACT.Copy, scale=b1_sb[:, 0:1]).then_inc(b1_spread, 1)
            act.wait_ge(w12_done, 1)
            act.copy(w12[:, :], w_ps[0:FEAT, 0:FEAT]).then_inc(w12_copied, 1)
            act.copy(c_rep[:, :], w_ps[:, FEAT:2 * FEAT]).then_inc(w12_copied, 1)
            act.wait_ge(edge_step, 3)
            act.copy(edge_blk[0:EP, :], digit_i[1][0:EP, :]).then_inc(edge_cast, 1)
            act.copy(ramp[:, :], ramp_i[:, :]).then_inc(ramps_cast, 1)
            act.copy(tile_no[:, :], tile_no_i[:, :]).then_inc(ramps_cast, 1)
            with act.Fori(0, PAIRS) as i:
                for b in range(2):
                    act.wait_ge(emb_multiplied, i * 2 + (b + 1))
                    act.copy(piece_of(i, b).rearrange("p (k t) f -> p k (t f)", k=2),
                             ps[:, 2 * b:2 * b + 2, 0:EB * FEAT]).then_inc(emb_copied, 1)
            with act.Fori(0, CHUNKS) as c:
                act.wait_ge(hist_added, c * CB + (CB + 2))
                act.copy(counts[:, bass.ds(c * SLOTS, SLOTS)], count_ps).then_inc(counts_copied, 1)
            act.wait_ge(deg_step, 1)
            act.activation(dtmp[:, :], deg[:, :], ACT.Sqrt).then_inc(root_taken, 1)

            def split_parts(r):
                with act.Fori(0, PAIRS) as i:
                    for b in range(2):
                        act.wait_ge(scaled, i * 2 + (r * PIECES + b + 1))
                        act.wait_ge(table_written[r][b], i * 16)
                        if r:
                            act.wait_ge(table_written[0][b], 16 * PAIRS)
                        act.copy(split[:, b, :, 0, :], piece_of(i, b)).then_inc(part_hi, 1)
                    for b in range(2):
                        act.wait_ge(rest_hi, i * 2 + (r * PIECES + b + 1))
                        act.copy(split[:, b, :, 1, :], rest[:, b, :, :]).then_inc(part_mid, 1)
                    for b in range(2):
                        act.wait_ge(rest_mid, i * 2 + (r * PIECES + b + 1))
                        act.copy(split[:, b, :, 2, :], rest[:, b, :, :]).then_inc(part_lo, 1)

            def scale_column(s, j):
                act.wait_ge(columns_placed, s * W8 + (j + 1))
                for k in range(2):
                    act.activation(piece[0:EP, k, j, :], prt_onehot[0:EP, :, j], ACT.Copy,
                                   scale=digit[k][0:EP, bass.ds(s * W8 + j, 1)]).then_inc(pieces_ready, 1)

            def stage_sources(g, total, h):
                for k in range(4 * h, 4 * h + 4):
                    act.wait_ge(gathered[k], total * 16)
                act.copy(source8[:, 4 * h:4 * h + 4], source[:, bass.ds(g * W8 + 4 * h, 4)]).then_inc(sources_staged, 1)

            split_parts(0)
            with act.Fori(0, CB) as i:
                act.wait_ge(rank_step, i * RANK + RANK)
                for j in range(W8):
                    scale_column(i, j)
            act.wait_ge(decode_step, DEC)
            for h in range(2):
                act.copy(source8[:, 4 * h:4 * h + 4], source[:, 4 * h:4 * h + 4]).then_inc(sources_staged, 1)
            with act.Fori(1, CHUNKS) as c:
                with act.Fori(0, CB) as i:
                    act.wait_ge(rank_step, (c * CB + i) * RANK + RANK)
                    for j in range(W8):
                        scale_column(c * CB + i, j)
                        if j % 4 == 3:
                            stage_sources((c - 1) * TB + i + 1, (c - 1) * TB + i + 1, j // 4)
                act.wait_ge(decode_step, c * DEC + DEC)
                with act.Fori(CB, TB) as i:
                    for h in range(2):
                        stage_sources((c - 1) * TB + i + 1, (c - 1) * TB + i + 1, h)
            with act.Fori((CHUNKS - 1) * TB + 1, BATCHES) as g:
                for h in range(2):
                    stage_sources(g, g, h)
            for h in range(2):
                stage_sources(0, BATCHES, h)
            split_parts(1)
            with act.Fori(1, BATCHES) as g:
                for h in range(2):
                    stage_sources(g, g + BATCHES, h)
            act.wait_ge(ask_step, ASK_STEPS)
            with act.Fori(0, OUT_ITERS) as i:
                for h in range(2):
                    act.wait_ge(rows_fetched[h], i * (16 * W8))
                    act.copy(ask8[:, h, :], ask_i[:, bass.ds(i * (2 * W8) + h * W8, W8)]).then_inc(asks_staged[h], 1)

        @block.tensor
        def _(pe):
            def clear(bank_ap):
                return pe.matmul(bank_ap, zeros[:, 0:P], zeros[:, 0:bank_ap.shape[1]], start=True, stop=False,
                                 skip_group_check=True)

            def add(dst, lhsT, rhs):
                return pe.matmul(dst, lhsT, rhs, start=False, stop=False, skip_group_check=True)

            pe.sem_inc(tiles_multiplied, CREDIT)
            pe.sem_inc(columns_placed, CREDIT)
            pe.sem_inc(hist_added, 2)
            pe.wait_ge(weights_loaded, 16 * 4)
            pe.wait_ge(b1_spread, 1)
            pe.matmul(w_ps[0:FEAT, 0:FEAT], w1_sb[:, :], w2_sb[:, :], start=True, stop=True)
            pe.matmul(w_ps[:, FEAT:2 * FEAT], b1_rep[:, :], w2_sb[:, :], start=True, stop=True).then_inc(w12_done, 1)
            pe.wait_ge(w12_copied, 2)
            with pe.Fori(0, PAIRS) as i:
                for b in range(2):
                    pe.wait_ge(emb_loaded[b], i * 16 + 16)
                    pe.wait_ge(emb_copied, i * 2 + (b + 1))
                    for k in range(PT):
                        last = pe.matmul(ps[:, 2 * b + k // EB, (k % EB) * FEAT:(k % EB + 1) * FEAT],
                                         emb_sb[:, b, k * P:(k + 1) * P], w12[:, :], start=True, stop=True)
                    last.then_inc(emb_multiplied, 1)
            clear(deg_ps)
            pe.wait_ge(triangles_made, 2)
            with pe.Fori(0, CHUNKS) as c:
                pe.wait_ge(counts_copied, c + 0)
                clear(count_ps)
                with pe.Fori(0, CB // 2) as i:
                    for b in range(2):
                        pe.wait_ge(hist_onehots, c * (2 * CB) + i * 4 + (2 * b + 2))
                        for j in range(W8):
                            add(deg_ps, lo_onehot[0:EP, b, :, j], hi_onehot[0:EP, b, :, j])
                        for k in range(BT):
                            last = add(count_ps, ones[0:EP, :],
                                       hi_onehot[0:EP, b, :, :].rearrange("p (n k) j -> p n k j", k=BT)[:, :, k, :])
                        last.then_inc(hist_added, 1)
            pe.wait_ge(emb_copied, PIECES + 2)
            clear(rank_ps).then_inc(rank_zeroed, 1)

            def rank_before(s):
                pe.wait_ge(blk_onehots, s + 1)
                add(rank_ps, before[0:EP, :], blk_onehot[0:EP, :, :]).then_inc(rank_summed, 1)

            def rank_rest(s):
                pe.wait_ge(rank_step, s * RANK + 1)
                add(rank_ps, not_before[0:EP, :], blk_onehot[0:EP, :, :]).then_inc(rank_advanced, 1)

            def place_column(s, j):
                pe.wait_ge(pieces_ready, s * (2 * W8) + (2 * j + 2))
                pe.wait_ge(tcol_onehots, s * W8 + (j + 1))
                for k in range(2):
                    last = add(place_ps[k], piece[0:EP, k, j, :], tcol_onehot[0:EP, j % RING, :])
                last.then_inc(columns_placed, 1)

            def multiply_tile(r, g, k):
                t = g * W8 + (r * BATCHES * W8 + k)
                pe.wait_ge(target_onehots, t + 1)
                pe.wait_ge(gathered[k], g * 16 + (r * BATCHES + 1) * 16)
                pe.wait_ge(tiles_added, t + (1 + CREDIT - RING))
                for n in range(BT):
                    for part in range(3):
                        last = pe.matmul(tile_ps[k % RING][:, n * FEAT:(n + 1) * FEAT],
                                         target_onehot[:, k % RING, n * P:(n + 1) * P],
                                         gath[:, k, part * FEAT:(part + 1) * FEAT],
                                         start=(part == 0), stop=(part == 2))
                last.then_inc(tiles_multiplied, 1)

            def open_chunk(c):
                pe.wait_ge(decode_step, c * DEC)
                pe.wait_ge(rank_seeded, c + 1)
                for k in range(2):
                    clear(place_ps[k])

            open_chunk(0)
            with pe.Fori(0, CB) as s:
                rank_before(s)
                rank_rest(s)
                for j in range(W8):
                    place_column(s, j)
            with pe.Fori(1, CHUNKS) as c:
                open_chunk(c)
                with pe.Fori(0, CB) as i:
                    for step in FUSED_PE:
                        if step[0] == "before":
                            rank_before(c * CB + i)
                        elif step[0] == "rest":
                            rank_rest(c * CB + i)
                        elif step[0] == "place":
                            place_column(c * CB + i, step[1])
                        else:
                            multiply_tile(0, (c - 1) * TB + i, step[1])
                with pe.Fori(CB, TB) as i:
                    for k in range(W8):
                        multiply_tile(0, (c - 1) * TB + i, k)
            with pe.Fori((CHUNKS - 1) * TB, BATCHES) as g:
                for k in range(W8):
                    multiply_tile(0, g, k)
            with pe.Fori(0, BATCHES) as g:
                for k in range(W8):
                    multiply_tile(1, g, k)

        @block.vector
        def _(dve):
            dve.sem_inc(emb_copied, 2)
            dve.sem_inc(tiles_added, CREDIT)

            def chain(step, first=0):
                n = [first]

                def link(ins):
                    n[0] += 1
                    ins.then_inc(step, 1)
                    dve.wait_ge(step, n[0])
                return link

            E = slice(0, EP)
            step = chain(edge_step)
            dve.wait_ge(cols_loaded, 16)
            step(dve.tensor_scalar(bits[E, :], cols[E, :], 7, None, ALU.logical_shift_right))
            step(dve.tensor_scalar(digit_i[0][E, :], cols[E, :], P - 1, None, ALU.bitwise_and))
            step(dve.tensor_scalar(digit_i[1][E, :], cols[E, :], 9, None, ALU.logical_shift_right))
            step(dve.tensor_scalar(cols[E, :], cols[E, :], BN - 1, None, ALU.bitwise_and))
            dve.wait_ge(rows_loaded, 16)
            dve.wait_ge(edge_cast, 1)
            step(dve.tensor_scalar(bits[E, :], rows[E, :], 7, None, ALU.logical_shift_right))
            step(dve.tensor_scalar(rows[E, :], rows[E, :], P - 1, None, ALU.bitwise_and))
            step(dve.scalar_tensor_tensor(rows[E, :], rows[E, :], float(NT), bits[E, :], ALU.mult, ALU.add))
            step(dve.tensor_scalar(bits[E, :], rows[E, :], 3, None, ALU.logical_shift_right))
            step(dve.tensor_scalar(rows[E, :], rows[E, :], 7, None, ALU.bitwise_and))
            dve.wait_ge(edge_cast, 3)
            step(dve.tensor_scalar(digit[0][E, :], bits[E, :], float(HALF), -float(CODE + 1), ALU.is_ge, ALU.mult))
            step(dve.scalar_tensor_tensor(digit[0][E, :], bits[E, :], 1.0, digit[0][E, :], ALU.add, ALU.add))
            step(dve.scalar_tensor_tensor(digit[1][E, :], rows[E, :], float(BN), cols[E, :], ALU.mult, ALU.add))
            step(dve.tensor_scalar(digit[1][E, :], digit[1][E, :], -float(HALF), None, ALU.add))

            dve.wait_ge(ramps_cast, 1)
            with dve.Fori(0, CHUNKS * CB // 2) as i:
                for b in range(2):
                    dve.wait_ge(hist_added, i * 2 + (b + 1))
                    for dst, src, width in ((hi_onehot, edge_hi, NT), (lo_onehot, edge_lo, P)):
                        dve.tensor_tensor(dst[E, b, :, :], ramp8[E, 0:width, :],
                                          src[E, bass.ds(i * (2 * W8) + b * W8, W8)].unsqueeze(1).broadcast_to([EP, width, W8]),
                                          ALU.is_equal).then_inc(hist_onehots, 1)

            step = chain(deg_step)
            dve.wait_ge(hist_added, CHUNKS * CB + 2)
            step(dve.tensor_scalar(deg[:, :], deg_ps, 1.0, 1.0, ALU.add, ALU.max))
            dve.wait_ge(root_taken, 1)
            step(dve.reciprocal(dinv[:, :], dtmp[:, :]))
            step(dve.tensor_tensor(dtmp[:, :], dinv[:, :], dinv[:, :], ALU.mult))
            step(dve.tensor_tensor(dtmp[:, :], dtmp[:, :], deg[:, :], ALU.mult))
            step(dve.tensor_scalar(dtmp[:, :], dtmp[:, :], -0.5, 1.5, ALU.mult, ALU.add))
            step(dve.tensor_tensor(dinv[:, :], dinv[:, :], dtmp[:, :], ALU.mult))

            def scale_piece(r, i, b):
                part = piece_of(i, b)
                by = dinv[:, bass.ds((i * 2 + b) * PT, PT)].unsqueeze(2).broadcast_to([P, PT, FEAT])
                if r:
                    n = i * 4 + 2 * b
                    dve.tensor_tensor(part, part, by, ALU.mult).then_inc(scale_step, 1)
                    dve.wait_ge(scale_step, n + 1)
                    dve.tensor_tensor(part, part, c_rep[:, :].unsqueeze(1).broadcast_to([P, PT, FEAT]),
                                      ALU.add).then_inc(scale_step, 1)
                    dve.wait_ge(scale_step, n + 2)
                dve.tensor_tensor(part, part, by, ALU.mult).then_inc(scaled, 1)

            def rest_piece(r, i, b):
                dve.wait_ge(part_mid, i * 2 + (r * PIECES + b + 1))
                dve.tensor_tensor(rest[:, b, :, :], rest[:, b, :, :], split[:, b, :, 1, :],
                                  ALU.subtract).then_inc(rest_mid, 1)

            def make_table(r):
                for b in range(2):
                    scale_piece(r, 0, b)
                with dve.Fori(1, PAIRS) as i:
                    for b in range(2):
                        scale_piece(r, i, b)
                    for b in range(2):
                        rest_piece(r, i - 1, b)
                for b in range(2):
                    rest_piece(r, PAIRS - 1, b)

            make_table(0)

            step = chain(base_step)
            dve.wait_ge(counts_copied, CHUNKS)
            dve.wait_ge(ramps_cast, 3)
            per_slot = counts[:, :].rearrange("p (n j) -> p n j", j=W8)
            flat = tot[:, :, :].rearrange("p c n -> p (c n)")
            flat_i = tot_i[:, :, :].rearrange("p c n -> p (c n)")
            step(dve.tensor_reduce(flat, per_slot, AX.X, ALU.add))
            step(dve.tensor_scalar(flat_i, flat, float(P - 1), None, ALU.add))
            step(dve.tensor_scalar(flat_i, flat_i, 7, None, ALU.logical_shift_right))
            step(dve.tensor_copy(flat, flat_i))
            for c in range(CHUNKS):
                step(dve.tensor_tensor_scan(endt[:, c, :], tot[:, c, :], zeros_f[:, 0:NB], 0.0, ALU.add, ALU.add))
                step(dve.tensor_tensor_scan(seed[:, c, :], counts[:, c * SLOTS:(c + 1) * SLOTS], zeros_f[:, 0:SLOTS],
                                            0.0, ALU.add, ALU.add))
            seed_flat = seed[:, :, :].rearrange("p c s -> p (c s)")
            seed_slot = seed[:, :, :].rearrange("p c (n j) -> p (c n) j", j=W8)
            step(dve.tensor_tensor(seed_flat, seed_flat, counts[:, :], ALU.subtract))
            step(dve.tensor_tensor(flat, endt[:, :, :].rearrange("p c n -> p (c n)"), flat, ALU.subtract))
            step(dve.scalar_tensor_tensor(flat, flat, float(P), seed_slot[:, :, 0], ALU.mult, ALU.subtract))
            step(dve.tensor_tensor(seed_slot, seed_slot, flat.unsqueeze(2).broadcast_to([P, CHUNKS * NB, W8]), ALU.add))
            step(dve.tensor_tensor(ended[:, :, :, :], endt[:, :, :].unsqueeze(2).broadcast_to([P, CHUNKS, BT, NB]),
                                   tile_no[:, :].unsqueeze(1).unsqueeze(3).broadcast_to([P, CHUNKS, BT, NB]), ALU.is_le))
            step(dve.tensor_reduce(blk_f[:, :], ended[:, :, :, :].rearrange("p c k n -> p (c k) n"), AX.X, ALU.add))
            step(dve.tensor_scalar(blk_i[:, :], blk_f[:, :], float(NB - 1), None, ALU.min))

            step = chain(ask_step)
            dve.wait_ge(ask_loaded, 16)
            step(dve.tensor_scalar(ask_f[:, :], ask_i[:, :], 0.0, float(NODES), ALU.is_lt, ALU.mult))
            step(dve.tensor_tensor(ask_f[:, :], ask_f[:, :], ask_i[:, :], ALU.add))
            step(dve.tensor_scalar(ask_t[0][:, :], ask_f[:, :], 0.0, float(NODES - 1), ALU.max, ALU.min))
            step(dve.tensor_scalar(ask_t[1][:, :], ask_t[0][:, :], 7, None, ALU.logical_shift_right))
            step(dve.tensor_scalar(ask_t[0][:, :], ask_t[0][:, :], P - 1, None, ALU.bitwise_and))
            step(dve.scalar_tensor_tensor(ask_i[:, :], ask_t[0][:, :], float(NT), ask_t[1][:, :], ALU.mult, ALU.add))

            block_of = [dve.alloc_register(f"block_of_{k}") for k in range(W8)]

            def seed_ranks(c):
                dve.wait_ge(rank_advanced, c * CB)
                dve.wait_ge(decode_step, c * DEC)
                dve.tensor_copy(rank_ps, seed_flat[:, bass.ds(c * SLOTS, SLOTS)]).then_inc(rank_seeded, 1)

            def block_onehots(s):
                dve.wait_ge(rank_advanced, s + 0)
                dve.tensor_tensor(blk_onehot[E, :, :], ramp8[E, 0:NB, :],
                                  edge_blk[E, bass.ds(s * W8, W8)].unsqueeze(1).broadcast_to([EP, NB, W8]),
                                  ALU.is_equal).then_inc(blk_onehots, 1)

            def pick_ranks(s):
                dve.wait_ge(rank_summed, s + 1)
                dve.tensor_tensor(picked[E, :, :], rank_ps[E, :].rearrange("p (n j) -> p n j", j=W8),
                                  blk_onehot[E, :, :], ALU.mult).then_inc(rank_step, 1)

            def sum_ranks(s):
                dve.wait_ge(rank_step, s * RANK + 1)
                with nc.allow_low_precision(reason="one whole number among zeros"):
                    dve.tensor_reduce(place_i[E, 0, :], picked[E, :, :].rearrange("p n j -> p j n"), AX.X,
                                      ALU.add).then_inc(rank_step, 1)

            def cut_places(s):
                dve.wait_ge(rank_step, s * RANK + 2)
                dve.tensor_scalar(place_i[E, 1, :], place_i[E, 0, :], 7, None, ALU.logical_shift_right).then_inc(rank_step, 1)
                dve.tensor_scalar(place_i[E, 2, :], place_i[E, 0, :], P - 1, None, ALU.bitwise_and).then_inc(rank_step, 1)

            def cast_places(s):
                dve.wait_ge(rank_step, s * RANK + 4)
                dve.tensor_copy(prt16[E, :], place_i[E, 2, :]).then_inc(rank_step, 1)
                dve.tensor_copy(tcol[E, :], place_i[E, 1, :]).then_inc(rank_step, 1)

            def partition_onehots(s):
                dve.wait_ge(rank_step, s * RANK + 6)
                dve.wait_ge(pieces_ready, s * (2 * W8))
                dve.tensor_tensor(prt_onehot[E, :, :], ramp8[E, 0:P, :],
                                  prt16[E, :].unsqueeze(1).broadcast_to([EP, P, W8]), ALU.is_equal).then_inc(rank_step, 1)

            def column_onehot(s, j):
                dve.wait_ge(columns_placed, s * W8 + (j + 1 + CREDIT - RING))
                dve.tensor_scalar(tcol_onehot[E, j % RING, :], ramp[E, 0:CT], tcol[E, j:j + 1], None,
                                  ALU.is_equal).then_inc(tcol_onehots, 1)

            def start_tiles(r, g):
                dve.wait_ge(target_onehots, g * W8 + r * BATCHES * W8)
                dve.tensor_copy(target8[:, :], target[:, bass.ds(g * W8, W8)]).then_inc(targets_staged, 1)
                dve.load(block_of, blocks[0:1, bass.ds(g * W8, W8)])

            def target_onehot_of(r, g, k):
                if k == 0:
                    dve.wait_ge(targets_staged, g + (r * BATCHES + 1))
                dve.wait_ge(tiles_multiplied, g * W8 + (r * BATCHES * W8 + k + 1 + CREDIT - RING))
                dve.tensor_scalar(target_onehot[:, k % RING, :], ramp[:, :], target8[:, k:k + 1], None,
                                  ALU.is_equal).then_inc(target_onehots, 1)

            def add_tile(r, g, k):
                t = g * W8 + (r * BATCHES * W8 + k)
                dve.wait_ge(tiles_multiplied, t + (1 + CREDIT))
                dve.wait_ge(tiles_added, t + CREDIT)
                blk = dve.snap(block_of[k], min_val=0, max_val=NB - 1)
                dst = acc[:, bass.ds(blk * BT, BT), :]
                dve.tensor_tensor(dst, dst, tile_ps[k % RING].rearrange("p (n f) -> p n f", f=FEAT),
                                  ALU.add).then_inc(tiles_added, 1)

            def tile_batch(r, g):
                start_tiles(r, g)
                for k in range(2):
                    target_onehot_of(r, g, k)
                for k in range(2, W8):
                    target_onehot_of(r, g, k)
                    add_tile(r, g, k - 2)
                for k in range(W8 - 2, W8):
                    add_tile(r, g, k)

            def decode(c):
                dve.wait_ge(columns_placed, c * (CB * W8) + (CB * W8 + CREDIT))
                n = [0]

                def link(ins):
                    n[0] += 1
                    ins.then_inc(decode_step, 1)
                    if n[0] < DEC:
                        dve.wait_ge(decode_step, c * DEC + n[0])
                link(dve.tensor_scalar(dec[0][:, :], place_ps[0], 0.0, float(CODE + 1), ALU.is_lt, ALU.mult))
                link(dve.tensor_tensor(dec[0][:, :], dec[0][:, :], place_ps[0], ALU.add))
                link(dve.tensor_scalar(dec_i[0][:, :], place_ps[1], float(HALF), None, ALU.add))
                link(dve.tensor_scalar(dec_i[1][:, :], dec_i[0][:, :], 9, None, ALU.logical_shift_right))
                link(dve.tensor_scalar(dec_i[0][:, :], dec_i[0][:, :], BN - 1, None, ALU.bitwise_and))
                link(dve.scalar_tensor_tensor(dec[1][:, :], dec[0][:, :], float(CODE // BN), dec_i[1][:, :], ALU.mult, ALU.add))
                link(dve.tensor_scalar(source[:, bass.ds(c * CT, CT)], dec[1][:, :], -float(CODE // BN), 0.0, ALU.add, ALU.max))
                link(dve.tensor_scalar(dec[1][:, :], dec[0][:, :], 0.0, NOWHERE, ALU.is_equal, ALU.mult))
                link(dve.tensor_tensor(target[:, bass.ds(c * CT, CT)], dec[1][:, :], dec_i[0][:, :], ALU.add))

            dve.wait_ge(rank_zeroed, 1)
            dve.wait_ge(ramps_cast, 3)
            seed_ranks(0)
            with dve.Fori(0, CB) as s:
                block_onehots(s)
                pick_ranks(s)
                sum_ranks(s)
                cut_places(s)
                cast_places(s)
                partition_onehots(s)
                for j in range(W8):
                    column_onehot(s, j)
            decode(0)
            dve.wait_ge(blocks_loaded, 16)
            with dve.Fori(1, CHUNKS) as c:
                seed_ranks(c)
                with dve.Fori(0, CB) as i:
                    s, g = c * CB + i, (c - 1) * TB + i
                    start_tiles(0, g)
                    for step in FUSED_DVE:
                        {"blocks": block_onehots, "pick": pick_ranks, "sum": sum_ranks, "cut": cut_places,
                         "cast": cast_places, "partitions": partition_onehots}[step[0]](s) if len(step) == 1 else (
                            column_onehot(s, step[1]) if step[0] == "column" else
                            target_onehot_of(0, g, step[1]) if step[0] == "target" else
                            add_tile(0, g, step[1]))
                decode(c)
                with dve.Fori(CB, TB) as i:
                    tile_batch(0, (c - 1) * TB + i)
            dve.wait_ge(decode_step, CHUNKS * DEC)
            with dve.Fori((CHUNKS - 1) * TB, BATCHES) as g:
                tile_batch(0, g)
            dve.wait_ge(tiles_added, BATCHES * W8 + CREDIT)
            make_table(1)
            with dve.Fori(0, BATCHES) as g:
                tile_batch(1, g)
            dve.wait_ge(tiles_added, 2 * BATCHES * W8 + CREDIT)
            for q in range(4):
                part = acc[:, q * QT:(q + 1) * QT, :]
                dve.tensor_tensor(part, part, dinv[:, q * QT:(q + 1) * QT].unsqueeze(2).broadcast_to([P, QT, FEAT]),
                                  ALU.mult).then_inc(lookup_scaled, 1)
                dve.wait_ge(lookup_scaled, 2 * q + 1)
                dve.tensor_tensor(part, part, b2_rep[:, :].unsqueeze(1).broadcast_to([P, QT, FEAT]),
                                  ALU.add).then_inc(lookup_scaled, 1)


FUSED_DVE = [("blocks",), ("target", 0), ("target", 1), ("pick",), ("target", 2), ("sum",), ("add", 0), ("cut",),
             ("target", 3), ("cast",), ("add", 1), ("partitions",),
             ("column", 0), ("target", 4), ("add", 2), ("column", 1), ("column", 2), ("target", 5), ("add", 3),
             ("column", 3), ("target", 6), ("add", 4), ("column", 4), ("column", 5), ("target", 7), ("add", 5),
             ("column", 6), ("add", 6), ("column", 7), ("add", 7)]
FUSED_PE = [("before",), ("tile", 0), ("rest",), ("tile", 1), ("tile", 2), ("tile", 3), ("place", 0), ("tile", 4),
            ("place", 1), ("place", 2), ("tile", 5), ("place", 3), ("tile", 6), ("place", 4), ("place", 5),
            ("tile", 7), ("place", 6), ("place", 7)]
BASE_STEPS = 4 + 2 * CHUNKS + 4 + 3
ASK_STEPS = 6


def kernel(**inputs):
    import numpy as np
    import concourse.bacc as bacc
    from concourse.bass_utils import run_bass_kernel_spmd

    emb = np.asarray(inputs["L0_rec_emb"])
    embT = np.zeros((FEAT, NT * P), emb.dtype)
    embT[:, 0:NODES] = emb.T
    arrays = {
        "r_input": np.ascontiguousarray(np.asarray(inputs["r_input"]).reshape(-1)),
        "edge_index": np.ascontiguousarray(inputs["L0_rec_edge_index"]),
        "embT": embT,
        "W1T": np.ascontiguousarray(np.asarray(inputs["L0_rec_W1"]).T),
        "b1": np.ascontiguousarray(inputs["L0_rec_b1"]),
        "W2": np.ascontiguousarray(inputs["L0_rec_W2"]),
        "b2": np.ascontiguousarray(inputs["L0_rec_b2"]),
    }
    nc = bacc.Bacc("TRN2", target_bir_lowering=False, num_devices=1)
    args = [nc.dram_tensor(name, a.shape, mybir.dt.from_np(a.dtype), kind="ExternalInput").ap() for name, a in arrays.items()]
    args.append(nc.dram_tensor("out", [LOOKUPS, FEAT], F32, kind="ExternalOutput").ap())
    build(nc, *args)
    r = run_bass_kernel_spmd(nc, [arrays], core_ids=[0])
    return r.results[0]["out"].reshape(512, 200, FEAT)
```

```python
from contextlib import ExitStack

import concourse.bass as bass
from concourse import mybir

F32 = mybir.dt.float32
BF16 = mybir.dt.bfloat16
F16 = mybir.dt.float16
I32 = mybir.dt.int32
ALU = mybir.AluOpType
ACT = mybir.ActivationFunctionType
AX = mybir.AxisListType

P = 128
NODES, FEAT, HID, EDGES = 25000, 64, 128, 250000
LOOKUPS = 512 * 200
NT = -(-NODES // P)
BT = 4
NB = NT // BT
BN = BT * P
EP = 125
EC = EDGES // EP
CHUNKS = 5
W8 = 8
CB = EC // CHUNKS // W8
CT = -(-((EC // CHUNKS * EP + NB * (P - 1)) // P) // W8) * W8
TB = CT // W8
TAIL = TB - CB
SLOTS = NB * W8
CODE = 4096
HALF = CODE // 2
PIECES, PT = 14, NT // 14
OUT_TILES = LOOKUPS // P
OUT_ITERS = OUT_TILES // (2 * W8)
GROUPS = NT // BT
CREDIT = 8
RING = 4
ON_ACT = (3, 6)
ON_DVE = W8 - len(ON_ACT)
NOWHERE = 600.0

assert NT % BT == 0 and CT <= 512 and CB * W8 * CHUNKS == EC and TAIL > 0
assert PIECES * PT == NT and OUT_ITERS * 2 * W8 == OUT_TILES
assert P * NT * BN < CODE * CODE and CB % 2 == 0 and GROUPS == CB - 1 and PT * 2 == 7 * BT


def dve_rank(k):
    return k - sum(m < k for m in ON_ACT)


def build(nc, r_input, edge_index, embT, W1T, b1, W2, b2, out):
    with ExitStack() as ctx:
        def sb(name, shape, dt):
            return ctx.enter_context(nc.sbuf_tensor(name, shape, dt))

        def sem(name):
            return ctx.enter_context(nc.semaphore(name))

        table = [nc.dram_tensor(f"table{r}", [P * NT, 3 * FEAT], BF16).ap() for r in range(2)]
        lookup = nc.dram_tensor("lookup", [P * NT, FEAT], F32).ap()
        blocks_dram = nc.dram_tensor("blocks_dram", [CHUNKS, P * BT], I32).ap()

        acc = sb("acc", [P, NT, FEAT], F32)
        edge_hi = sb("edge_hi", [P, EC], F16)
        edge_lo = sb("edge_lo", [P, EC], F16)
        edge_blk = sb("edge_blk", [P, EC], F16)
        digit = [sb(f"digit{k}", [P, EC], F32) for k in range(2)]
        digit_i = [d[:, :].bitcast(I32) for d in digit]
        scratch = sb("scratch", [P, 3 * EC], I32)
        rows, cols, bits = (scratch[:, k * EC:(k + 1) * EC] for k in range(3))
        SPN = PT * FEAT
        split = scratch[:, 0:2 * 3 * SPN // 2].bitcast(BF16).rearrange(
            "p (b t c f) -> p b t c f", b=2, t=PT, c=3)
        rest = scratch[:, 3 * SPN:3 * SPN + 2 * SPN].bitcast(F32).rearrange(
            "p (b t f) -> p b t f", b=2, t=PT)
        ramp8 = sb("ramp8", [P, 256, W8], F16)
        ramp = sb("ramp", [P, BN], F16)
        zeros_f = sb("zeros_f", [P, 512], F32)
        zeros = zeros_f[:, 0:256].bitcast(F16)
        ones = sb("ones", [P, P], F16)
        before = sb("before", [P, P], F16)
        not_before = sb("not_before", [P, P], F16)
        hi_onehot = sb("hi_onehot", [P, 2, NT, W8], F16)
        lo_onehot = sb("lo_onehot", [P, 2, P, W8], F16)
        late = sb("late", [P, RING * CT + 2 * W8 * P + RING * BN + W8 * 3 * FEAT], F16)
        w1_sb = sb("w1_sb", [HID, FEAT], F32)
        w2_sb = sb("w2_sb", [HID, FEAT], F32)
        b1_sb = sb("b1_sb", [HID, 1], F32)
        b1_rep = sb("b1_rep", [HID, P], F32)
        b2_rep = sb("b2_rep", [P, FEAT], F32)
        w12 = sb("w12", [FEAT, FEAT], F32)
        c_rep = sb("c_rep", [P, FEAT], F32)
        deg = sb("deg", [P, NT], F32)
        dinv = sb("dinv", [P, NT], F32)
        dtmp = sb("dtmp", [P, NT], F32)
        counts = sb("counts", [P, CHUNKS * SLOTS], F32)
        seed = sb("seed", [P, CHUNKS, SLOTS], F32)
        tot = sb("tot", [P, CHUNKS, NB], F32)
        tot_i = sb("tot_i", [P, CHUNKS, NB], I32)
        endt = sb("endt", [P, CHUNKS, NB], F32)
        tile_no_i = sb("tile_no_i", [P, BT], I32)
        tile_no = sb("tile_no", [P, BT], F32)
        ended = scratch[:, 5 * SPN:5 * SPN + CHUNKS * BT * NB].bitcast(F32).rearrange(
            "p (c k n) -> p c k n", c=CHUNKS, k=BT)
        blk_f = sb("blk_f", [P, CHUNKS * BT], F32)
        blk_i = sb("blk_i", [P, CHUNKS * BT], I32)
        blocks = sb("blocks", [1, CHUNKS * CT], I32)
        blk_onehot = sb("blk_onehot", [P, NB, W8], F16)
        picked = sb("picked", [P, NB, W8], F32)
        place_i = sb("place_i", [P, 2, W8], I32)
        prt16 = sb("prt16", [P, W8], F16)
        tcol = sb("tcol", [P, 2, W8], I32)
        prt_onehot = sb("prt_onehot", [P, 2, P, W8], F16)
        at = [0, RING * CT, RING * CT + 2 * W8 * P, RING * CT + 2 * W8 * P + RING * BN]
        tcol_onehot = late[:, at[0]:at[1]].rearrange("p (r t) -> p r t", r=RING)
        piece = late[:, at[1]:at[2]].rearrange("p (k j m) -> p k j m", k=2, j=W8)
        dec = [sb(f"dec{k}", [P, CT], F32) for k in range(2)]
        dec_i = [sb(f"dec_i{k}", [P, CT], I32) for k in range(2)]
        source = sb("source", [P, CHUNKS * CT], I32)
        target = sb("target", [P, CHUNKS * CT], F32)
        source8 = sb("source8", [P, W8], I32)
        target8 = sb("target8", [P, W8], F32)
        target_onehot = late[:, at[2]:at[3]].rearrange("p (r n) -> p r n", r=RING)
        emb_sb = late[0:FEAT, at[2]:at[3]].bitcast(F32).rearrange("p (b n) -> p b n", b=2)
        distance = sb("distance", [P, BN], F16)
        one_col = sb("one_col", [P, 1], F32)
        gath = late[:, at[3]:].bitcast(BF16).rearrange("p (k f) -> p k f", k=W8)
        ramp8_i = source[:, 0:256 * W8].rearrange("p (w j) -> p w j", j=W8)
        ramp_i = target[:, 0:BN].bitcast(I32)
        ask_i = sb("ask_i", [P, OUT_TILES], I32)
        ask_t = late[:, 0:2 * OUT_TILES].bitcast(I32)
        ask_f = late[:, 2 * OUT_TILES:4 * OUT_TILES].bitcast(F32)
        ask8 = sb("ask8", [P, 2, W8], I32)
        out_rows = sb("out_rows", [P, 2, W8, FEAT], F32)

        ps = ctx.enter_context(nc.psum_tensor("ps", [P, 8, 512], F32))
        rank_ps = ps[:, 0, 0:SLOTS]
        place_ps = [ps[:, 1 + k, 0:CT] for k in range(2)]
        tile_ps = [ps[:, 3 + k, 0:BT * FEAT] for k in range(RING)]
        deg_ps = ps[:, 6, 0:NT]
        count_ps = ps[:, 7, 0:SLOTS]
        emb_ps = [ps[:, 3 + k, 0:BT * FEAT] for k in range(2)]
        w_ps = ps[:, 4, :]

        cols_loaded = sem("cols_loaded")
        rows_loaded = sem("rows_loaded")
        weights_loaded = sem("weights_loaded")
        ask_loaded = sem("ask_loaded")
        emb_loaded = [sem(f"emb_loaded{k}") for k in range(2)]
        ints_made = sem("ints_made")
        triangles_made = sem("triangles_made")
        ramps_cast = sem("ramps_cast")
        b1_spread = sem("b1_spread")
        w12_done = sem("w12_done")
        w12_copied = sem("w12_copied")
        emb_multiplied = sem("emb_multiplied")
        emb_scaled = sem("emb_scaled")
        edge_step = sem("edge_step")
        edge_cast = sem("edge_cast")
        hist_onehots = sem("hist_onehots")
        degrees_added = sem("degrees_added")
        hist_added = sem("hist_added")
        chunk_counted = sem("chunk_counted")
        counts_copied = sem("counts_copied")
        deg_copied = sem("deg_copied")
        deg_step = sem("deg_step")
        root_taken = sem("root_taken")
        base_step = sem("base_step")
        blocks_stored = sem("blocks_stored")
        blocks_loaded = sem("blocks_loaded")
        rank_zeroed = sem("rank_zeroed")
        rank_seeded = sem("rank_seeded")
        blk_onehots = sem("blk_onehots")
        rank_summed = sem("rank_summed")
        rank_advanced = sem("rank_advanced")
        rank_step = sem("rank_step")
        pieces_ready = sem("pieces_ready")
        tcol_onehots = sem("tcol_onehots")
        columns_placed = sem("columns_placed")
        decode_step = sem("decode_step")
        sources_staged = sem("sources_staged")
        targets_staged = sem("targets_staged")
        target_onehots = sem("target_onehots")
        act_onehots = sem("act_onehots")
        distances = sem("distances")
        part_step = sem("part_step")
        gathered = [sem(f"gathered{k}") for k in range(W8)]
        waits_passed = sem("waits_passed")
        tiles_multiplied = sem("tiles_multiplied")
        tiles_added = sem("tiles_added")
        scale_step = sem("scale_step")
        scaled = sem("scaled")
        part_hi = sem("part_hi")
        rest_hi = sem("rest_hi")
        part_mid = sem("part_mid")
        rest_mid = sem("rest_mid")
        part_lo = sem("part_lo")
        table_written = [sem(f"table_written{b}") for b in range(2)]
        ask_step = sem("ask_step")
        lookup_scaled = sem("lookup_scaled")
        pool_scaled = sem("pool_scaled")
        lookup_written = sem("lookup_written")
        asks_staged = [sem(f"asks_staged{h}") for h in range(2)]
        rows_fetched = [sem(f"rows_fetched{h}") for h in range(2)]
        out_written = [sem(f"out_written{h}") for h in range(2)]

        BATCHES = CHUNKS * TB
        RANK = 6
        DEC = 9
        PARTS = 4
        PAIRS = PIECES // 2

        table_v = [t.rearrange("(p i) f -> p i f", p=P) for t in table]
        lookup_v = lookup.rearrange("(p i) f -> p i f", p=P)
        QT = NT // 4

        def scale_lookup(eng, q, step):
            part = acc[:, q * QT:(q + 1) * QT, :]
            done = 2 * q if step is lookup_scaled else 0
            eng.tensor_tensor(part, part, dinv[:, q * QT:(q + 1) * QT].unsqueeze(2).broadcast_to([P, QT, FEAT]),
                              ALU.mult).then_inc(step, 1)
            eng.wait_ge(step, done + 1)
            eng.tensor_tensor(part, part, b2_rep[:, :].unsqueeze(1).broadcast_to([P, QT, FEAT]),
                              ALU.add).then_inc(step, 1)

        def piece_of(i, b):
            return acc[:, bass.ds((i * 2 + b) * PT, PT), :]

        block = ctx.enter_context(nc.Block())

        @block.sync
        def _(sp):
            ei = edge_index.rearrange("a (p c) -> a p c", p=EP)
            sp.dma_start(cols[0:EP, :], ei[1]).then_inc(cols_loaded, 16)
            sp.dma_start(w1_sb[:, :], W1T).then_inc(weights_loaded, 16)
            sp.dma_start(w2_sb[:, :], W2).then_inc(weights_loaded, 16)
            sp.dma_start(b1_sb[:, :], b1.rearrange("(p a) -> p a", a=1)).then_inc(weights_loaded, 16)
            sp.dma_start(b2_rep[:, :], b2.rearrange("(a f) -> a f", a=1).broadcast_to([P, FEAT])).then_inc(weights_loaded, 16)
            for b in range(2):
                sp.dma_start(emb_sb[:, b, :], embT[:, b * BN:(b + 1) * BN]).then_inc(emb_loaded[b], 16)
            sp.dma_start(rows[0:EP, :], ei[0]).then_inc(rows_loaded, 16)
            sp.dma_start(ask_i[:, :], r_input.rearrange("(p t) -> p t", p=P)).then_inc(ask_loaded, 16)
            def write_table(r):
                with sp.Fori(0, PAIRS) as i:
                    for b in range(2):
                        sp.wait_ge(part_lo, i * 2 + (r * PIECES + b + 1))
                        sp.dma_start(table_v[r][:, bass.ds((i * 2 + b) * PT, PT), :],
                                     split[:, b, :, :, :].rearrange("p t c f -> p t (c f)")).then_inc(table_written[b], 16)

            sp.wait_ge(base_step, BASE_STEPS)
            sp.dma_start(blocks_dram.rearrange("c (p k) -> p c k", p=P),
                         blk_i[:, :].rearrange("p (c k) -> p c k", c=CHUNKS)).then_inc(blocks_stored, 16)
            sp.wait_ge(blocks_stored, 16)
            sp.dma_start(blocks[0:1, :].rearrange("a (c t) -> a c t", c=CHUNKS),
                         blocks_dram[:, 0:CT].rearrange("(a c) t -> a c t", a=1)).then_inc(blocks_loaded, 16)
            write_table(0)
            write_table(1)
            for q in range(4):
                if q < 3:
                    sp.wait_ge(lookup_scaled, 2 * (q + 1))
                else:
                    sp.wait_ge(pool_scaled, 2)
                sp.dma_start(lookup_v[:, q * QT:(q + 1) * QT, :], acc[:, q * QT:(q + 1) * QT, :]).then_inc(lookup_written, 16)
            out_v = out.rearrange("(p t) f -> p t f", p=P)
            with sp.Fori(0, OUT_ITERS) as i:
                for h in range(2):
                    sp.wait_ge(rows_fetched[h], i * (16 * W8) + 16 * W8)
                    sp.dma_start(out_v[:, bass.ds(i * (2 * W8) + h * W8, W8), :], out_rows[:, h, :, :]).then_inc(out_written[h], 16)
            for h in range(2):
                sp.wait_ge(out_written[h], 16 * OUT_ITERS)

        @block.gpsimd
        def _(pool):
            pool.iota(ramp8_i[:, :, :], pattern=[[1, 256], [0, W8]], base=0, channel_multiplier=0).then_inc(ints_made, 1)
            pool.memset(zeros_f[:, :], 0.0).then_inc(ints_made, 1)
            pool.memset(ones[:, :], 1.0).then_inc(ints_made, 1)
            pool.memset(one_col[:, :], 1.0).then_inc(ints_made, 1)
            pool.iota(ramp_i[:, :], pattern=[[1, BN]], base=0, channel_multiplier=0).then_inc(ints_made, 1)
            pool.iota(tile_no_i[:, :], pattern=[[1, BT]], base=0, channel_multiplier=BT).then_inc(ints_made, 1)
            pool.wait_ge(ints_made, 6)
            pool.affine_select(out=before[:, :], in_=ones[:, :], compare_op=ALU.is_gt, fill=0.0,
                               base=0, pattern=[[1, P]], channel_multiplier=-1).then_inc(triangles_made, 1)
            pool.affine_select(out=not_before[:, :], in_=ones[:, :], compare_op=ALU.is_ge, fill=0.0,
                               base=0, pattern=[[-1, P]], channel_multiplier=1).then_inc(triangles_made, 1)
            def pool_piece(i, b):
                pool.wait_ge(emb_scaled, i * 7 + (4 + 3 * b + 2))
                if not isinstance(i, int):
                    pool.wait_ge(table_written[b], i * 16)
                pool.sem_inc(waits_passed, 1)
                done = i * (2 * PARTS) + b * PARTS
                pool.tensor_copy(split[:, b, :, 0, :], piece_of(i, b)).then_inc(part_step, 1)
                pool.wait_ge(part_step, done + 1)
                pool.sem_inc(waits_passed, 1)
                pool.tensor_tensor(rest[:, b, :, :], piece_of(i, b), split[:, b, :, 0, :], ALU.subtract).then_inc(part_step, 1)
                pool.wait_ge(part_step, done + 2)
                pool.sem_inc(waits_passed, 1)
                pool.tensor_copy(split[:, b, :, 1, :], rest[:, b, :, :]).then_inc(part_step, 1)
                pool.wait_ge(part_step, done + 3)
                pool.sem_inc(waits_passed, 1)
                pool.tensor_tensor(rest[:, b, :, :], rest[:, b, :, :], split[:, b, :, 1, :], ALU.subtract).then_inc(part_step, 1)
                pool.wait_ge(part_step, done + 4)
                pool.sem_inc(waits_passed, 1)
                pool.tensor_copy(split[:, b, :, 2, :], rest[:, b, :, :]).then_inc(part_lo, 1)

            for b in range(2):
                pool_piece(0, b)
            with pool.Fori(1, PAIRS) as i:
                for b in range(2):
                    pool_piece(i, b)
            for r in range(2):
                if r == 1:
                    with pool.Fori(0, PAIRS) as i:
                        for b in range(2):
                            pool.wait_ge(part_hi, i * 2 + (b + 1))
                            pool.tensor_tensor(rest[:, b, :, :], piece_of(i, b), split[:, b, :, 0, :],
                                               ALU.subtract).then_inc(rest_hi, 1)
                for b in range(2):
                    pool.wait_ge(table_written[b], 16 * PAIRS * (r + 1))
                with pool.Fori(0, BATCHES) as g:
                    for k in range(W8):
                        if k % 4 == 0:
                            pool.wait_ge(sources_staged, g * 2 + (2 * r * BATCHES + 1 + k // 4))
                        pool.wait_ge(tiles_multiplied, g * W8 + (r * BATCHES * W8 + k + 1))
                        pool.sem_inc(waits_passed, 1)
                        pool.indirect_dma_start(
                            out=gath[:, k, :], out_offset=None, in_=table[r],
                            in_offset=bass.IndirectOffsetOnAxis(ap=source8[:, k:k + 1], axis=0)).then_inc(gathered[k], 16)
            pool.wait_ge(tiles_added, 2 * BATCHES * W8 + CREDIT)
            scale_lookup(pool, 3, pool_scaled)
            pool.wait_ge(lookup_written, 16 * 4)

            def fetch_half(i, h):
                pool.wait_ge(asks_staged[h], i + 1)
                if not isinstance(i, int):
                    pool.wait_ge(out_written[h], i * 16)
                pool.sem_inc(waits_passed, 1)
                for k in range(W8):
                    pool.indirect_dma_start(
                        out=out_rows[:, h, k, :], out_offset=None, in_=lookup,
                        in_offset=bass.IndirectOffsetOnAxis(ap=ask8[:, h, k:k + 1], axis=0)).then_inc(rows_fetched[h], 16)

            for h in range(2):
                fetch_half(0, h)
            with pool.Fori(1, OUT_ITERS) as i:
                for h in range(2):
                    fetch_half(i, h)

        @block.scalar
        def _(act):
            act.wait_ge(ints_made, 6)
            act.copy(ramp8[:, :, :], ramp8_i[:, :, :]).then_inc(ramps_cast, 1)
            act.wait_ge(edge_step, 1)
            act.copy(edge_hi[0:EP, :], bits[0:EP, :]).then_inc(edge_cast, 1)
            act.wait_ge(edge_step, 2)
            act.copy(edge_lo[0:EP, :], digit_i[0][0:EP, :]).then_inc(edge_cast, 1)
            act.wait_ge(weights_loaded, 16 * 4)
            act.activation(b1_rep[:, :], ones[:, :], ACT.Copy, scale=b1_sb[:, 0:1]).then_inc(b1_spread, 1)
            act.wait_ge(w12_done, 1)
            act.copy(w12[:, :], w_ps[0:FEAT, 0:FEAT]).then_inc(w12_copied, 1)
            act.copy(c_rep[:, :], w_ps[:, FEAT:2 * FEAT]).then_inc(w12_copied, 1)
            act.wait_ge(edge_step, 3)
            act.copy(edge_blk[0:EP, :], digit_i[1][0:EP, :]).then_inc(edge_cast, 1)
            act.copy(ramp[:, :], ramp_i[:, :]).then_inc(ramps_cast, 1)
            act.copy(tile_no[:, :], tile_no_i[:, :]).then_inc(ramps_cast, 1)
            with act.Fori(0, CHUNKS) as c:
                act.wait_ge(hist_added, c * CB + (CB + 2))
                act.copy(counts[:, bass.ds(c * SLOTS, SLOTS)], count_ps).then_inc(counts_copied, 1)
            act.wait_ge(deg_step, 1)
            act.activation(dtmp[:, :], deg[:, :], ACT.Sqrt).then_inc(root_taken, 1)

            def split_parts():
                with act.Fori(0, PAIRS) as i:
                    for b in range(2):
                        act.wait_ge(scaled, i * 2 + (b + 1))
                        act.wait_ge(table_written[b], i * 16 + 16 * PAIRS)
                        act.copy(split[:, b, :, 0, :], piece_of(i, b)).then_inc(part_hi, 1)
                    for b in range(2):
                        act.wait_ge(rest_hi, i * 2 + (b + 1))
                        act.copy(split[:, b, :, 1, :], rest[:, b, :, :]).then_inc(part_mid, 1)
                    for b in range(2):
                        act.wait_ge(rest_mid, i * 2 + (b + 1))
                        act.copy(split[:, b, :, 2, :], rest[:, b, :, :]).then_inc(part_lo, 1)

            def scale_column(s, j, b):
                act.wait_ge(columns_placed, s * W8 + (j + 1))
                for k in range(2):
                    act.activation(piece[0:EP, k, j, :], prt_onehot[0:EP, b, :, j], ACT.Copy,
                                   scale=digit[k][0:EP, bass.ds(s * W8 + j, 1)]).then_inc(pieces_ready, 1)

            def act_onehot(r, g, k):
                n = g * len(ON_ACT) + (r * BATCHES * len(ON_ACT) + ON_ACT.index(k))
                if k == ON_ACT[0]:
                    act.wait_ge(targets_staged, g + (r * BATCHES + 1))
                act.wait_ge(act_onehots, n + 1)
                act.activation(distance[:, :], ramp[:, :], ACT.Abs, bias=target8[:, k:k + 1], scale=-1.0).then_inc(distances, 1)
                act.wait_ge(distances, n + 1)
                act.wait_ge(tiles_multiplied, g * W8 + (r * BATCHES * W8 + k + 1 + CREDIT - RING))
                act.activation(target_onehot[:, k % RING, :], distance[:, :], ACT.Relu, bias=one_col[:, 0:1],
                               scale=-1.0).then_inc(act_onehots, 1)

            def stage_sources(g, total, h):
                for k in range(4 * h, 4 * h + 4):
                    act.wait_ge(gathered[k], total * 16)
                act.copy(source8[:, 4 * h:4 * h + 4], source[:, bass.ds(g * W8 + 4 * h, 4)]).then_inc(sources_staged, 1)

            def sort_batch(s, b, load):
                act.wait_ge(rank_step, s * RANK + RANK)
                for j in range(W8):
                    scale_column(s, j, b)
                    if load and j == W8 - 2:
                        act.wait_ge(emb_multiplied, s + 1)
                        act.dma_start(emb_sb[:, b, :], embT[:, bass.ds((s + 2) * BN, BN)]).then_inc(emb_loaded[b], 16)

            with act.Fori(0, (GROUPS - 3) // 2) as i:
                for b in range(2):
                    sort_batch(i * 2 + b, b, True)
            for s in range(GROUPS - 3, CB):
                sort_batch(s, s % 2, s + 2 < GROUPS)
            act.wait_ge(decode_step, DEC)
            for h in range(2):
                act.copy(source8[:, 4 * h:4 * h + 4], source[:, 4 * h:4 * h + 4]).then_inc(sources_staged, 1)

            def tile_batch(r, g, then):
                for h in range(2):
                    act_onehot(r, g, ON_ACT[h])
                    if then is not None:
                        stage_sources(then, g + (r * BATCHES + 1), h)

            with act.Fori(1, CHUNKS) as c:
                with act.Fori(0, CB // 2) as i:
                    for b in range(2):
                        s = c * CB + i * 2 + b
                        g = (c - 1) * TB + i * 2 + b
                        act_onehot(0, g, ON_ACT[0])
                        act.wait_ge(rank_step, s * RANK + RANK)
                        for j in range(W8):
                            scale_column(s, j, b)
                            if j == 1:
                                stage_sources(g + 1, g + 1, 0)
                            if j == 3:
                                act_onehot(0, g, ON_ACT[1])
                        stage_sources(g + 1, g + 1, 1)
                act.wait_ge(decode_step, c * DEC + DEC)
                with act.Fori(CB, TB) as i:
                    tile_batch(0, (c - 1) * TB + i, (c - 1) * TB + i + 1)
            with act.Fori((CHUNKS - 1) * TB, BATCHES - 1) as g:
                tile_batch(0, g, g + 1)
            tile_batch(0, BATCHES - 1, 0)
            split_parts()
            with act.Fori(0, BATCHES - 1) as g:
                tile_batch(1, g, g + 1)
            tile_batch(1, BATCHES - 1, None)
            act.wait_ge(ask_step, ASK_STEPS)
            for h in range(2):
                act.copy(ask8[:, h, :], ask_i[:, h * W8:(h + 1) * W8]).then_inc(asks_staged[h], 1)
            with act.Fori(1, OUT_ITERS) as i:
                for h in range(2):
                    act.wait_ge(rows_fetched[h], i * (16 * W8))
                    act.copy(ask8[:, h, :], ask_i[:, bass.ds(i * (2 * W8) + h * W8, W8)]).then_inc(asks_staged[h], 1)

        @block.tensor
        def _(pe):
            def clear(bank_ap):
                return pe.matmul(bank_ap, zeros[:, 0:P], zeros[:, 0:bank_ap.shape[1]], start=True, stop=False,
                                 skip_group_check=True)

            def add(dst, lhsT, rhs):
                return pe.matmul(dst, lhsT, rhs, start=False, stop=False, skip_group_check=True)

            pe.sem_inc(tiles_multiplied, CREDIT)
            pe.sem_inc(columns_placed, CREDIT)
            pe.sem_inc(hist_added, 2)
            pe.sem_inc(degrees_added, 2)
            pe.sem_inc(rank_advanced, 1)
            pe.wait_ge(weights_loaded, 16 * 4)
            pe.wait_ge(b1_spread, 1)
            pe.matmul(w_ps[0:FEAT, 0:FEAT], w1_sb[:, :], w2_sb[:, :], start=True, stop=True)
            pe.matmul(w_ps[:, FEAT:2 * FEAT], b1_rep[:, :], w2_sb[:, :], start=True, stop=True).then_inc(w12_done, 1)
            pe.wait_ge(w12_copied, 2)
            clear(deg_ps)
            pe.wait_ge(triangles_made, 2)
            with pe.Fori(0, CHUNKS) as c:
                pe.wait_ge(counts_copied, c + 1)
                clear(count_ps)
                with pe.Fori(0, CB // 2) as i:
                    for b in range(2):
                        pe.wait_ge(hist_onehots, c * (2 * CB) + i * 4 + (2 * b + 2))
                        for j in range(W8):
                            last = add(deg_ps, lo_onehot[0:EP, b, :, j], hi_onehot[0:EP, b, :, j])
                        last.then_inc(degrees_added, 1)
                        for k in range(BT):
                            last = add(count_ps, ones[0:EP, :],
                                       hi_onehot[0:EP, b, :, :].rearrange("p (n k) j -> p n k j", k=BT)[:, :, k, :])
                        last.then_inc(hist_added, 1)
            clear(rank_ps).then_inc(rank_zeroed, 1)

            def rank_before(s):
                pe.wait_ge(blk_onehots, s + 1)
                add(rank_ps, before[0:EP, :], blk_onehot[0:EP, :, :]).then_inc(rank_summed, 1)

            def rank_rest(s):
                pe.wait_ge(rank_step, s * RANK + 1)
                add(rank_ps, not_before[0:EP, :], blk_onehot[0:EP, :, :]).then_inc(rank_advanced, 1)

            def place_column(s, j):
                pe.wait_ge(pieces_ready, s * (2 * W8) + (2 * j + 2 + PIECE_CREDIT))
                pe.wait_ge(tcol_onehots, s * W8 + (j + 1))
                for k in range(2):
                    last = add(place_ps[k], piece[0:EP, k, j, :], tcol_onehot[0:EP, j % RING, :])
                last.then_inc(columns_placed, 1)

            def multiply_tile(r, g, k):
                t = g * W8 + (r * BATCHES * W8 + k)
                if k in ON_ACT:
                    pe.wait_ge(act_onehots, g * len(ON_ACT) + (r * BATCHES * len(ON_ACT) + ON_ACT.index(k) + 2))
                else:
                    pe.wait_ge(target_onehots, g * ON_DVE + (r * BATCHES * ON_DVE + dve_rank(k) + 2))
                pe.wait_ge(gathered[k], g * 16 + (r * BATCHES + 1) * 16)
                pe.wait_ge(tiles_added, t + (1 + CREDIT - RING))
                for n in range(BT):
                    for part in range(3):
                        last = pe.matmul(tile_ps[k % RING][:, n * FEAT:(n + 1) * FEAT],
                                         target_onehot[:, k % RING, n * P:(n + 1) * P],
                                         gath[:, k, part * FEAT:(part + 1) * FEAT],
                                         start=(part == 0), stop=(part == 2))
                last.then_inc(tiles_multiplied, 1)

            def open_chunk(c):
                if not isinstance(c, int):
                    pe.wait_ge(decode_step, c * DEC)
                pe.wait_ge(rank_seeded, c + 1)
                for k in range(2):
                    clear(place_ps[k])

            open_chunk(0)
            rank_before(0)
            rank_rest(0)

            def sort_batch(i, b):
                s = i * 2 + b
                rank_before(s + 1)
                place_column(s, 0)
                rank_rest(s + 1)
                place_column(s, 1)
                pe.wait_ge(emb_loaded[b], i * 16 + 16)
                pe.wait_ge(emb_scaled, s + 1)
                for k in range(BT):
                    last = pe.matmul(emb_ps[b][:, k * FEAT:(k + 1) * FEAT], emb_sb[:, b, k * P:(k + 1) * P], w12[:, :],
                                     start=True, stop=True)
                last.then_inc(emb_multiplied, 1)
                for j in range(2, W8):
                    place_column(s, j)

            with pe.Fori(0, CB // 2 - 1) as i:
                for b in range(2):
                    sort_batch(i, b)
            sort_batch(CB // 2 - 1, 0)
            for j in range(W8):
                place_column(CB - 1, j)
            with pe.Fori(1, CHUNKS) as c:
                open_chunk(c)
                rank_before(c * CB)
                rank_rest(c * CB)

                def both(at, more):
                    s, g = c * CB + at, (c - 1) * TB + at
                    if more:
                        rank_before(s + 1)
                    for k in range(W8):
                        multiply_tile(0, g, k)
                        place_column(s, k)
                        if more and k == 0:
                            rank_rest(s + 1)

                with pe.Fori(0, CB // 2 - 1) as i:
                    for b in range(2):
                        both(i * 2 + b, True)
                both(CB - 2, True)
                both(CB - 1, False)
                with pe.Fori(CB, TB) as i:
                    for k in range(W8):
                        multiply_tile(0, (c - 1) * TB + i, k)
            with pe.Fori((CHUNKS - 1) * TB, BATCHES) as g:
                for k in range(W8):
                    multiply_tile(0, g, k)
            with pe.Fori(0, BATCHES) as g:
                for k in range(W8):
                    multiply_tile(1, g, k)

        @block.vector
        def _(dve):
            dve.sem_inc(emb_scaled, 2)
            dve.sem_inc(counts_copied, 1)
            dve.sem_inc(pieces_ready, PIECE_CREDIT)
            dve.sem_inc(target_onehots, 1)
            dve.sem_inc(act_onehots, 1)
            dve.sem_inc(tiles_added, CREDIT)

            def chain(step, first=0):
                n = [first]

                def link(ins):
                    n[0] += 1
                    ins.then_inc(step, 1)
                    dve.wait_ge(step, n[0])
                return link

            E = slice(0, EP)
            step = chain(edge_step)
            dve.wait_ge(cols_loaded, 16)
            step(dve.tensor_scalar(bits[E, :], cols[E, :], 7, None, ALU.logical_shift_right))
            step(dve.tensor_scalar(digit_i[0][E, :], cols[E, :], P - 1, None, ALU.bitwise_and))
            step(dve.tensor_scalar(digit_i[1][E, :], cols[E, :], 9, None, ALU.logical_shift_right))
            step(dve.tensor_scalar(cols[E, :], cols[E, :], BN - 1, None, ALU.bitwise_and))
            dve.wait_ge(rows_loaded, 16)
            dve.wait_ge(edge_cast, 1)
            step(dve.tensor_scalar(bits[E, :], rows[E, :], 7, None, ALU.logical_shift_right))
            step(dve.tensor_scalar(rows[E, :], rows[E, :], P - 1, None, ALU.bitwise_and))
            step(dve.scalar_tensor_tensor(rows[E, :], rows[E, :], float(NT), bits[E, :], ALU.mult, ALU.add))
            step(dve.tensor_scalar(bits[E, :], rows[E, :], 3, None, ALU.logical_shift_right))
            step(dve.tensor_scalar(rows[E, :], rows[E, :], 7, None, ALU.bitwise_and))
            dve.wait_ge(edge_cast, 3)
            step(dve.tensor_scalar(digit[0][E, :], bits[E, :], float(HALF), -float(CODE + 1), ALU.is_ge, ALU.mult))
            step(dve.scalar_tensor_tensor(digit[0][E, :], bits[E, :], 1.0, digit[0][E, :], ALU.add, ALU.add))
            step(dve.scalar_tensor_tensor(digit[1][E, :], rows[E, :], float(BN), cols[E, :], ALU.mult, ALU.add))
            step(dve.tensor_scalar(digit[1][E, :], digit[1][E, :], -float(HALF), None, ALU.add))

            dve.wait_ge(ramps_cast, 1)
            with dve.Fori(0, CHUNKS * CB // 2) as i:
                for b in range(2):
                    for dst, src, width, used in ((lo_onehot, edge_lo, P, degrees_added), (hi_onehot, edge_hi, NT, hist_added)):
                        dve.wait_ge(used, i * 2 + (b + 1))
                        dve.tensor_tensor(dst[E, b, :, :], ramp8[E, 0:width, :],
                                          src[E, bass.ds(i * (2 * W8) + b * W8, W8)].unsqueeze(1).broadcast_to([EP, width, W8]),
                                          ALU.is_equal).then_inc(hist_onehots, 1)

            step = chain(deg_step)
            dve.wait_ge(hist_added, CHUNKS * CB + 2)
            step(dve.tensor_scalar(deg[:, :], deg_ps, 1.0, 1.0, ALU.add, ALU.max))
            dve.wait_ge(root_taken, 1)
            step(dve.reciprocal(dinv[:, :], dtmp[:, :]))
            step(dve.tensor_tensor(dtmp[:, :], dinv[:, :], dinv[:, :], ALU.mult))
            step(dve.tensor_tensor(dtmp[:, :], dtmp[:, :], deg[:, :], ALU.mult))
            step(dve.tensor_scalar(dtmp[:, :], dtmp[:, :], -0.5, 1.5, ALU.mult, ALU.add))
            step(dve.tensor_tensor(dinv[:, :], dinv[:, :], dtmp[:, :], ALU.mult))

            def scale_piece(i, b):
                part = piece_of(i, b)
                by = dinv[:, bass.ds((i * 2 + b) * PT, PT)].unsqueeze(2).broadcast_to([P, PT, FEAT])
                n = i * 4 + 2 * b
                dve.tensor_tensor(part, part, by, ALU.mult).then_inc(scale_step, 1)
                dve.wait_ge(scale_step, n + 1)
                dve.tensor_tensor(part, part, c_rep[:, :].unsqueeze(1).broadcast_to([P, PT, FEAT]),
                                  ALU.add).then_inc(scale_step, 1)
                dve.wait_ge(scale_step, n + 2)
                dve.tensor_tensor(part, part, by, ALU.mult).then_inc(scaled, 1)

            def rest_piece(i, b):
                dve.wait_ge(part_mid, i * 2 + (b + 1))
                dve.tensor_tensor(rest[:, b, :, :], rest[:, b, :, :], split[:, b, :, 1, :],
                                  ALU.subtract).then_inc(rest_mid, 1)

            def make_table():
                for b in range(2):
                    scale_piece(0, b)
                with dve.Fori(1, PAIRS) as i:
                    for b in range(2):
                        scale_piece(i, b)
                    for b in range(2):
                        rest_piece(i - 1, b)
                for b in range(2):
                    rest_piece(PAIRS - 1, b)

            step = chain(base_step)
            dve.wait_ge(counts_copied, CHUNKS + 1)
            dve.wait_ge(ramps_cast, 3)
            per_slot = counts[:, :].rearrange("p (n j) -> p n j", j=W8)
            flat = tot[:, :, :].rearrange("p c n -> p (c n)")
            flat_i = tot_i[:, :, :].rearrange("p c n -> p (c n)")
            step(dve.tensor_reduce(flat, per_slot, AX.X, ALU.add))
            step(dve.tensor_scalar(flat_i, flat, float(P - 1), None, ALU.add))
            step(dve.tensor_scalar(flat_i, flat_i, 7, None, ALU.logical_shift_right))
            step(dve.tensor_copy(flat, flat_i))
            for c in range(CHUNKS):
                step(dve.tensor_tensor_scan(endt[:, c, :], tot[:, c, :], zeros_f[:, 0:NB], 0.0, ALU.add, ALU.add))
                step(dve.tensor_tensor_scan(seed[:, c, :], counts[:, c * SLOTS:(c + 1) * SLOTS], zeros_f[:, 0:SLOTS],
                                            0.0, ALU.add, ALU.add))
            seed_flat = seed[:, :, :].rearrange("p c s -> p (c s)")
            seed_slot = seed[:, :, :].rearrange("p c (n j) -> p (c n) j", j=W8)
            step(dve.tensor_tensor(seed_flat, seed_flat, counts[:, :], ALU.subtract))
            step(dve.tensor_tensor(flat, endt[:, :, :].rearrange("p c n -> p (c n)"), flat, ALU.subtract))
            step(dve.scalar_tensor_tensor(flat, flat, float(P), seed_slot[:, :, 0], ALU.mult, ALU.subtract))
            step(dve.tensor_tensor(seed_slot, seed_slot, flat.unsqueeze(2).broadcast_to([P, CHUNKS * NB, W8]), ALU.add))
            step(dve.tensor_tensor(ended[:, :, :, :], endt[:, :, :].unsqueeze(2).broadcast_to([P, CHUNKS, BT, NB]),
                                   tile_no[:, :].unsqueeze(1).unsqueeze(3).broadcast_to([P, CHUNKS, BT, NB]), ALU.is_le))
            step(dve.tensor_reduce(blk_f[:, :], ended[:, :, :, :].rearrange("p c k n -> p (c k) n"), AX.X, ALU.add))
            step(dve.tensor_scalar(blk_i[:, :], blk_f[:, :], float(NB - 1), None, ALU.min))

            def find_asked():
                step = chain(ask_step)
                dve.wait_ge(ask_loaded, 16)
                step(dve.tensor_scalar(ask_f, ask_i[:, :], 0.0, float(NODES), ALU.is_lt, ALU.mult))
                step(dve.tensor_tensor(ask_f, ask_f, ask_i[:, :], ALU.add))
                step(dve.tensor_scalar(ask_t, ask_f, 0.0, float(NODES - 1), ALU.max, ALU.min))
                step(dve.tensor_scalar(ask_i[:, :], ask_t, 7, None, ALU.logical_shift_right))
                step(dve.tensor_scalar(ask_t, ask_t, P - 1, None, ALU.bitwise_and))
                step(dve.scalar_tensor_tensor(ask_i[:, :], ask_t, float(NT), ask_i[:, :], ALU.mult, ALU.add))

            block_of = [dve.alloc_register(f"block_of_{k}") for k in range(W8)]

            def seed_ranks(c):
                dve.wait_ge(rank_advanced, c * CB + 1)
                dve.tensor_copy(rank_ps, seed_flat[:, bass.ds(c * SLOTS, SLOTS)]).then_inc(rank_seeded, 1)

            def block_onehots(s):
                dve.wait_ge(rank_advanced, s + 1)
                dve.tensor_tensor(blk_onehot[E, :, :], ramp8[E, 0:NB, :],
                                  edge_blk[E, bass.ds(s * W8, W8)].unsqueeze(1).broadcast_to([EP, NB, W8]),
                                  ALU.is_equal).then_inc(blk_onehots, 1)

            def pick_ranks(s):
                dve.wait_ge(rank_summed, s + 1)
                dve.tensor_tensor(picked[E, :, :], rank_ps[E, :].rearrange("p (n j) -> p n j", j=W8),
                                  blk_onehot[E, :, :], ALU.mult).then_inc(rank_step, 1)

            def sum_ranks(s):
                dve.wait_ge(rank_step, s * RANK + 1)
                with nc.allow_low_precision(reason="one whole number among zeros"):
                    dve.tensor_reduce(place_i[E, 0, :], picked[E, :, :].rearrange("p n j -> p j n"), AX.X,
                                      ALU.add).then_inc(rank_step, 1)

            def cut_places(s, b):
                dve.wait_ge(rank_step, s * RANK + 2)
                dve.tensor_scalar(place_i[E, 1, :], place_i[E, 0, :], P - 1, None, ALU.bitwise_and).then_inc(rank_step, 1)
                dve.tensor_scalar(tcol[E, b, :], place_i[E, 0, :], 7, None, ALU.logical_shift_right).then_inc(rank_step, 1)

            def cast_places(s):
                dve.wait_ge(rank_step, s * RANK + 3)
                dve.tensor_copy(prt16[E, :], place_i[E, 1, :]).then_inc(rank_step, 1)

            def partition_onehots(s, b):
                dve.wait_ge(rank_step, s * RANK + 5)
                dve.wait_ge(pieces_ready, s * (2 * W8) + (PIECE_CREDIT - 2 * W8))
                dve.tensor_tensor(prt_onehot[E, b, :, :], ramp8[E, 0:P, :],
                                  prt16[E, :].unsqueeze(1).broadcast_to([EP, P, W8]), ALU.is_equal).then_inc(rank_step, 1)

            def column_onehot(s, j, b):
                dve.wait_ge(columns_placed, s * W8 + (j + 1 + CREDIT - RING))
                dve.tensor_scalar(tcol_onehot[E, j % RING, :], ramp[E, 0:CT], tcol[E, b, j:j + 1], None,
                                  ALU.is_equal).then_inc(tcol_onehots, 1)

            def stage_targets(g, total):
                dve.wait_ge(target_onehots, total * ON_DVE + 1)
                dve.wait_ge(act_onehots, total * len(ON_ACT) + 1)
                dve.tensor_copy(target8[:, :], target[:, bass.ds(g * W8, W8)]).then_inc(targets_staged, 1)

            def load_blocks(g):
                dve.load(block_of, blocks[0:1, bass.ds(g * W8, W8)])

            def target_onehot_of(r, g, k):
                if k in ON_ACT:
                    return
                if k == 0:
                    dve.wait_ge(targets_staged, g + (r * BATCHES + 1))
                dve.wait_ge(tiles_multiplied, g * W8 + (r * BATCHES * W8 + k + 1 + CREDIT - RING))
                dve.tensor_scalar(target_onehot[:, k % RING, :], ramp[:, :], target8[:, k:k + 1], None,
                                  ALU.is_equal).then_inc(target_onehots, 1)

            def add_tile(r, g, k):
                t = g * W8 + (r * BATCHES * W8 + k)
                dve.wait_ge(tiles_multiplied, t + (1 + CREDIT))
                dve.wait_ge(tiles_added, t + CREDIT)
                blk = dve.snap(block_of[k], min_val=0, max_val=NB - 1)
                dst = acc[:, bass.ds(blk * BT, BT), :]
                dve.tensor_tensor(dst, dst, tile_ps[k % RING].rearrange("p (n f) -> p n f", f=FEAT),
                                  ALU.add).then_inc(tiles_added, 1)

            def tile_batch(r, g, then, decoded=None):
                for k in range(3):
                    target_onehot_of(r, g, k)
                load_blocks(g)
                add_tile(r, g, 0)
                for k in range(3, W8):
                    target_onehot_of(r, g, k)
                    add_tile(r, g, k - 2)
                add_tile(r, g, W8 - 2)
                if decoded is not None:
                    dve.wait_ge(decode_step, decoded * DEC + DEC)
                if then is not None:
                    stage_targets(then, g + (r * BATCHES + 1))
                add_tile(r, g, W8 - 1)

            def decode(c):
                dve.wait_ge(columns_placed, c * (CB * W8) + (CB * W8 + CREDIT))
                n = [0]

                def link(ins):
                    n[0] += 1
                    ins.then_inc(decode_step, 1)
                    if n[0] < DEC:
                        dve.wait_ge(decode_step, c * DEC + n[0])
                link(dve.tensor_scalar(dec[0][:, :], place_ps[0], 0.0, float(CODE + 1), ALU.is_lt, ALU.mult))
                link(dve.tensor_tensor(dec[0][:, :], dec[0][:, :], place_ps[0], ALU.add))
                link(dve.tensor_scalar(dec_i[0][:, :], place_ps[1], float(HALF), None, ALU.add))
                link(dve.tensor_scalar(dec_i[1][:, :], dec_i[0][:, :], 9, None, ALU.logical_shift_right))
                link(dve.tensor_scalar(dec_i[0][:, :], dec_i[0][:, :], BN - 1, None, ALU.bitwise_and))
                link(dve.scalar_tensor_tensor(dec[1][:, :], dec[0][:, :], float(CODE // BN), dec_i[1][:, :], ALU.mult, ALU.add))
                link(dve.tensor_scalar(source[:, bass.ds(c * CT, CT)], dec[1][:, :], -float(CODE // BN), 0.0, ALU.add, ALU.max))
                link(dve.tensor_scalar(dec[1][:, :], dec[0][:, :], 0.0, NOWHERE, ALU.is_equal, ALU.mult))
                link(dve.tensor_tensor(target[:, bass.ds(c * CT, CT)], dec[1][:, :], dec_i[0][:, :], ALU.add))

            dve.wait_ge(rank_zeroed, 1)
            dve.wait_ge(ramps_cast, 3)
            seed_ranks(0)
            def first_places(s):
                block_onehots(s)
                pick_ranks(s)
                sum_ranks(s)
                cut_places(s, 0)
                cast_places(s)
                partition_onehots(s, 0)

            first_places(0)

            def sort_batch(i, b):
                s = i * 2 + b
                block_onehots(s + 1)
                column_onehot(s, 0, b)
                pick_ranks(s + 1)
                column_onehot(s, 1, b)
                sum_ranks(s + 1)
                column_onehot(s, 2, b)
                cut_places(s + 1, 1 - b)
                column_onehot(s, 3, b)
                cast_places(s + 1)
                dve.wait_ge(emb_multiplied, s + 1)
                dve.tensor_tensor(acc[:, bass.ds(s * BT, BT), :], emb_ps[b].rearrange("p (t f) -> p t f", f=FEAT),
                                  dinv[:, bass.ds(s * BT, BT)].unsqueeze(2).broadcast_to([P, BT, FEAT]),
                                  ALU.mult).then_inc(emb_scaled, 1)
                partition_onehots(s + 1, 1 - b)
                for j in range(4, W8):
                    column_onehot(s, j, b)

            with dve.Fori(0, CB // 2 - 1) as i:
                for b in range(2):
                    sort_batch(i, b)
            sort_batch(CB // 2 - 1, 0)
            for j in range(W8):
                column_onehot(CB - 1, j, 1)
            decode(0)
            dve.wait_ge(blocks_loaded, 16)
            dve.wait_ge(decode_step, DEC)
            dve.tensor_copy(target8[:, :], target[:, 0:W8]).then_inc(targets_staged, 1)
            with dve.Fori(1, CHUNKS) as c:
                seed_ranks(c)
                first_places(c * CB)

                def both(at, b, first=False, last=False):
                    s, g = c * CB + at, (c - 1) * TB + at
                    for step in BOTH:
                        what, k = step[0], step[-1]
                        if what == "late add":
                            if not first:
                                add_tile(0, g - 1, k)
                        elif what == "stage":
                            stage_targets(g + 1, g + 1)
                        elif what == "column":
                            column_onehot(s, k, b)
                        elif what == "target":
                            target_onehot_of(0, g, k)
                        elif what == "add":
                            add_tile(0, g, k)
                        elif what == "load":
                            load_blocks(g)
                        elif last:
                            continue
                        elif what == "blocks":
                            block_onehots(s + 1)
                        elif what == "pick":
                            pick_ranks(s + 1)
                        elif what == "sum":
                            sum_ranks(s + 1)
                        elif what == "cut":
                            cut_places(s + 1, 1 - b)
                        elif what == "cast":
                            cast_places(s + 1)
                        elif what == "partitions":
                            partition_onehots(s + 1, 1 - b)

                both(0, 0, first=True)
                with dve.Fori(0, CB // 2 - 1) as i:
                    for b in range(2):
                        both(i * 2 + (1 + b), 1 - b)
                both(CB - 1, 1, last=True)
                for k in LATE:
                    add_tile(0, (c - 1) * TB + (CB - 1), k)
                decode(c)
                with dve.Fori(CB, TB) as i:
                    tile_batch(0, (c - 1) * TB + i, (c - 1) * TB + i + 1, decoded=c)
            with dve.Fori((CHUNKS - 1) * TB, BATCHES - 1) as g:
                tile_batch(0, g, g + 1)
            tile_batch(0, BATCHES - 1, 0)
            dve.wait_ge(tiles_added, BATCHES * W8 + CREDIT)
            make_table()
            find_asked()
            with dve.Fori(0, BATCHES - 1) as g:
                tile_batch(1, g, g + 1)
            tile_batch(1, BATCHES - 1, None)
            dve.wait_ge(tiles_added, 2 * BATCHES * W8 + CREDIT)
            for q in range(3):
                scale_lookup(dve, q, lookup_scaled)


BOTH = [("blocks",), ("target", 0), ("column", 0), ("late add", 6), ("target", 1), ("pick",), ("late add", 7),
        ("load",), ("column", 1), ("sum",), ("target", 2), ("column", 2), ("add", 0), ("cut",), ("column", 3), ("add", 1),
        ("cast",), ("target", 4), ("column", 4), ("add", 2), ("partitions",), ("target", 5), ("column", 5), ("add", 3),
        ("column", 6), ("add", 4), ("target", 7), ("column", 7), ("stage",), ("add", 5)]
LATE = [step[-1] for step in BOTH if step[0] == "late add"]
PIECE_CREDIT = 2 * 2 * W8
BASE_STEPS = 4 + 2 * CHUNKS + 4 + 3
ASK_STEPS = 6


def kernel(**inputs):
    import numpy as np
    import concourse.bacc as bacc
    from concourse.bass_utils import run_bass_kernel_spmd

    emb = np.asarray(inputs["L0_rec_emb"])
    embT = np.zeros((FEAT, NT * P), emb.dtype)
    embT[:, 0:NODES] = emb.T
    arrays = {
        "r_input": np.ascontiguousarray(np.asarray(inputs["r_input"]).reshape(-1)),
        "edge_index": np.ascontiguousarray(inputs["L0_rec_edge_index"]),
        "embT": embT,
        "W1T": np.ascontiguousarray(np.asarray(inputs["L0_rec_W1"]).T),
        "b1": np.ascontiguousarray(inputs["L0_rec_b1"]),
        "W2": np.ascontiguousarray(inputs["L0_rec_W2"]),
        "b2": np.ascontiguousarray(inputs["L0_rec_b2"]),
    }
    nc = bacc.Bacc("TRN2", target_bir_lowering=False, num_devices=1)
    args = [nc.dram_tensor(name, a.shape, mybir.dt.from_np(a.dtype), kind="ExternalInput").ap() for name, a in arrays.items()]
    args.append(nc.dram_tensor("out", [LOOKUPS, FEAT], F32, kind="ExternalOutput").ap())
    build(nc, *args)
    r = run_bass_kernel_spmd(nc, [arrays], core_ids=[0])
    return r.results[0]["out"].reshape(512, 200, FEAT)
```

```python
from contextlib import ExitStack

import concourse.bass as bass
from concourse import mybir

F32 = mybir.dt.float32
BF16 = mybir.dt.bfloat16
F16 = mybir.dt.float16
I32 = mybir.dt.int32
ALU = mybir.AluOpType
ACT = mybir.ActivationFunctionType
AX = mybir.AxisListType

P = 128
NODES, FEAT, HID, EDGES = 25000, 64, 128, 250000
LOOKUPS = 512 * 200
NT = -(-NODES // P)
BT = 4
NB = NT // BT
BN = BT * P
EP = 125
EC = EDGES // EP
CHUNKS = 5
W8 = 8
CB = EC // CHUNKS // W8
GB = -(-(EC // CHUNKS * EP) // (P * W8))
GT = GB * W8
CV = -(-(-(-(EC // CHUNKS * EP) // P) + NB - 1) // W8) * W8
VB = CV // W8
LAG = (NB - 1) // W8
RINGB = 2 * LAG + 2
RINGT = RINGB * W8
LEAD = LAG
HALF_RING = RINGB // 2
RECIPROCAL = (1 << 16) // RINGT + 1
SLOTS = NB * W8
CODE = 4096
HALF = CODE // 2
PIECES, PT = 14, NT // 14
OUT_TILES = LOOKUPS // P
OUT_ITERS = OUT_TILES // (2 * W8)
GROUPS = NT // BT
CREDIT = 8
VISIT_CREDIT = 2 * W8
RING = 4
ON_ACT = (3, 6)
ON_DVE = W8 - len(ON_ACT)
NOWHERE = 600.0

assert NT % BT == 0 and CV <= 512 and CB * W8 * CHUNKS == EC and CB < VB
assert PIECES * PT == NT and OUT_ITERS * 2 * W8 == OUT_TILES
assert P * NT * BN < CODE * CODE and GB == HALF_RING ** 2 and GB % 2 == 1 and VB == GB + LEAD and GB == CB - 1 and LAG * W8 == NB - 1
assert all(t * RECIPROCAL >> 16 == t // RINGT for t in range(GT + RINGT // 2))
assert CB % 2 == 0 and GROUPS == CB - 1 and PT * 2 == 7 * BT


def dve_rank(k):
    return k - sum(m < k for m in ON_ACT)


def build(nc, r_input, edge_index, embT, W1T, b1, W2, b2, out):
    with ExitStack() as ctx:
        def sb(name, shape, dt):
            return ctx.enter_context(nc.sbuf_tensor(name, shape, dt))

        def sem(name):
            return ctx.enter_context(nc.semaphore(name))

        table = [nc.dram_tensor(f"table{r}", [P * NT, 3 * FEAT], BF16).ap() for r in range(2)]
        lookup = nc.dram_tensor("lookup", [P * NT, FEAT], F32).ap()
        visits_dram = nc.dram_tensor("visits_dram", [2, CHUNKS, P * BT], I32).ap()

        acc = sb("acc", [P, NT, FEAT], F32)
        scratch = sb("scratch", [P, 5 * EC + 3 * EC // 2], I32)
        rows, cols, bits = (scratch[:, k * EC:(k + 1) * EC] for k in range(3))
        digit_i = [scratch[:, k * EC:(k + 1) * EC] for k in (3, 4)]
        digit = [d.bitcast(F32) for d in digit_i]
        edge_hi, edge_lo, edge_blk = (
            scratch[:, 5 * EC + k * EC // 2:5 * EC + (k + 1) * EC // 2].bitcast(F16) for k in range(3))
        SPN = PT * FEAT
        split = scratch[:, 0:2 * 3 * SPN // 2].bitcast(BF16).rearrange(
            "p (b t c f) -> p b t c f", b=2, t=PT, c=3)
        rest = scratch[:, 3 * SPN:3 * SPN + 2 * SPN].bitcast(F32).rearrange(
            "p (b t f) -> p b t f", b=2, t=PT)
        ramp8 = sb("ramp8", [P, 256, W8], F16)
        ramp = sb("ramp", [P, BN], F16)
        zeros_f = sb("zeros_f", [P, 512], F32)
        zeros = zeros_f[:, 0:256].bitcast(F16)
        ones = sb("ones", [P, P], F16)
        before = sb("before", [P, P], F16)
        not_before = sb("not_before", [P, P], F16)
        hi_onehot = sb("hi_onehot", [P, 2, NT, W8], F16)
        lo_onehot = sb("lo_onehot", [P, 2, P, W8], F16)
        late = sb("late", [P, RING * CV + 2 * W8 * P + RING * BN], F16)
        w1_sb = sb("w1_sb", [HID, FEAT], F32)
        w2_sb = sb("w2_sb", [HID, FEAT], F32)
        b1_sb = sb("b1_sb", [HID, 1], F32)
        b1_rep = sb("b1_rep", [HID, P], F32)
        b2_rep = sb("b2_rep", [P, FEAT], F32)
        w12 = sb("w12", [FEAT, FEAT], F32)
        c_rep = sb("c_rep", [P, FEAT], F32)
        deg = sb("deg", [P, NT], F32)
        dinv = sb("dinv", [P, NT], F32)
        dtmp = sb("dtmp", [P, NT], F32)
        counts = sb("counts", [P, CHUNKS * SLOTS], F32)
        seed = sb("seed", [P, CHUNKS, SLOTS], F32)
        tot = sb("tot", [P, CHUNKS, NB], F32)
        tot_i = sb("tot_i", [P, CHUNKS, NB], I32)
        endt = sb("endt", [P, CHUNKS, NB], F32)
        low = sb("low", [P, CHUNKS, NB], I32)
        low_f = low[:, :, :].bitcast(F32)
        visit_no_i = sb("visit_no_i", [P, BT], I32)
        visit_no = sb("visit_no", [P, BT], F32)
        ended = scratch[:, 5 * SPN:5 * SPN + CHUNKS * BT * NB].bitcast(F32).rearrange(
            "p (c k n) -> p c k n", c=CHUNKS, k=BT)
        blk_f = sb("blk_f", [P, CHUNKS * BT], F32)
        tile_of = sb("tile_of", [P, CHUNKS, BT], F32)
        tile_of_ring = sb("tile_of_ring", [P, CHUNKS, BT], F32)
        tile_i = sb("tile_i", [P, CHUNKS * BT], I32)
        visit_at = sb("visit_at", [P, 2, CHUNKS * BT], I32)
        visits = sb("visits", [2, CHUNKS * CV], I32)
        blk_onehot = sb("blk_onehot", [P, NB, W8], F16)
        picked = sb("picked", [P, NB, W8], F32)
        place_i = sb("place_i", [P, 2, W8], I32)
        prt16 = sb("prt16", [P, W8], F16)
        tcol = sb("tcol", [P, 2, W8], I32)
        prt_onehot = sb("prt_onehot", [P, 2, P, W8], F16)
        at = [0, RING * CV, RING * CV + 2 * W8 * P, RING * CV + 2 * W8 * P + RING * BN]
        tcol_onehot = late[:, at[0]:at[1]].rearrange("p (r t) -> p r t", r=RING)
        piece = late[:, at[1]:at[2]].rearrange("p (k j m) -> p k j m", k=2, j=W8)
        dec = [sb(f"dec{k}", [P, CV], F32) for k in range(2)]
        dec_i = [sb(f"dec_i{k}", [P, CV], I32) for k in range(2)]
        source = sb("source", [P, CHUNKS * CV], I32)
        target = sb("target", [P, CHUNKS * CV], F32)
        visit_source = lo_onehot[:, 0, :, :].rearrange("p m j -> p (m j)")[:, 0:2 * CV].bitcast(F32)
        turned = lo_onehot[:, 1, :, :].rearrange("p m j -> p (m j)").bitcast(F32)
        visit_tile = hi_onehot[:, :, :, :].rearrange("p b n j -> p (b n j)")[:, 0:2 * BT * GT].bitcast(F32).rearrange(
            "p (k t) -> p k t", k=BT)
        identity = sb("identity", [P, P], F32)
        source8 = sb("source8", [P, W8], I32)
        target8 = sb("target8", [P, W8], F32)
        target_onehot = late[:, at[2]:at[3]].rearrange("p (r n) -> p r n", r=RING)
        emb_sb = late[0:FEAT, at[2]:at[3]].bitcast(F32).rearrange("p (b n) -> p b n", b=2)
        distance = sb("distance", [P, BN], F16)
        one_col = sb("one_col", [P, 1], F32)
        gath = scratch[:, 0:RINGT * 3 * FEAT // 2].bitcast(BF16).rearrange("p (k f) -> p k f", k=RINGT)
        ramp8_i = acc[:, 0:256 * W8 // FEAT, :].bitcast(I32).rearrange("p t f -> p (t f)").rearrange(
            "p (w j) -> p w j", j=W8)
        ramp_i = target[:, 0:BN].bitcast(I32)
        visit_rows = late[:, at[1]:at[1] + W8 * 3 * FEAT].bitcast(BF16).rearrange("p (k f) -> p k f", k=W8)
        ask_i = sb("ask_i", [P, OUT_TILES], I32)
        ask_t = late[:, 0:2 * OUT_TILES].bitcast(I32)
        ask_f = late[:, 2 * OUT_TILES:4 * OUT_TILES].bitcast(F32)
        ask8 = sb("ask8", [P, 2, W8], I32)
        out_rows = sb("out_rows", [P, 2, W8, FEAT], F32)

        ps = ctx.enter_context(nc.psum_tensor("ps", [P, 8, 512], F32))
        rank_ps = ps[:, 0, 0:SLOTS]
        place_ps = [ps[:, 1 + k, 0:CV] for k in range(2)]
        visit_ps = [ps[:, 3 + k, 0:BT * FEAT] for k in range(RING)]
        deg_ps = ps[:, 6, 0:NT]
        count_ps = ps[:, 7, 0:SLOTS]
        emb_ps = [ps[:, 3 + k, 0:BT * FEAT] for k in range(2)]
        w_ps = ps[:, 4, :]
        tiles_ps = ps[:, 6, 0:GT]
        turned_ps = ps[0:CV // BT, 7, :]

        cols_loaded = sem("cols_loaded")
        rows_loaded = sem("rows_loaded")
        weights_loaded = sem("weights_loaded")
        ask_loaded = sem("ask_loaded")
        emb_loaded = [sem(f"emb_loaded{k}") for k in range(2)]
        ints_made = sem("ints_made")
        triangles_made = sem("triangles_made")
        ramps_cast = sem("ramps_cast")
        b1_spread = sem("b1_spread")
        w12_done = sem("w12_done")
        w12_copied = sem("w12_copied")
        emb_multiplied = sem("emb_multiplied")
        emb_scaled = sem("emb_scaled")
        edge_step = sem("edge_step")
        edge_cast = sem("edge_cast")
        hist_onehots = sem("hist_onehots")
        degrees_added = sem("degrees_added")
        hist_added = sem("hist_added")
        counts_copied = sem("counts_copied")
        deg_step = sem("deg_step")
        root_taken = sem("root_taken")
        base_step = sem("base_step")
        identity_made = sem("identity_made")
        visits_stored = sem("visits_stored")
        visits_loaded = sem("visits_loaded")
        visit_tiles = sem("visit_tiles")
        turned_made = sem("turned_made")
        turned_copied = sem("turned_copied")
        tiles_made = sem("tiles_made")
        sources_spread = sem("sources_spread")
        sources_ready = sem("sources_ready")
        rank_zeroed = sem("rank_zeroed")
        rank_seeded = sem("rank_seeded")
        blk_onehots = sem("blk_onehots")
        rank_summed = sem("rank_summed")
        rank_advanced = sem("rank_advanced")
        rank_step = sem("rank_step")
        pieces_ready = sem("pieces_ready")
        tcol_onehots = sem("tcol_onehots")
        columns_placed = sem("columns_placed")
        decode_step = sem("decode_step")
        sources_staged = sem("sources_staged")
        targets_staged = sem("targets_staged")
        target_onehots = sem("target_onehots")
        act_onehots = sem("act_onehots")
        distances = sem("distances")
        part_step = sem("part_step")
        gathered = [sem(f"gathered{k}") for k in range(W8)]
        waits_passed = sem("waits_passed")
        rows_copied = sem("rows_copied")
        visits_multiplied = sem("visits_multiplied")
        visits_added = sem("visits_added")
        scale_step = sem("scale_step")
        scaled = sem("scaled")
        part_hi = sem("part_hi")
        rest_hi = sem("rest_hi")
        part_mid = sem("part_mid")
        rest_mid = sem("rest_mid")
        part_lo = sem("part_lo")
        table_written = [sem(f"table_written{b}") for b in range(2)]
        ask_step = sem("ask_step")
        lookup_scaled = sem("lookup_scaled")
        pool_scaled = sem("pool_scaled")
        lookup_written = sem("lookup_written")
        asks_staged = [sem(f"asks_staged{h}") for h in range(2)]
        rows_fetched = [sem(f"rows_fetched{h}") for h in range(2)]
        out_written = [sem(f"out_written{h}") for h in range(2)]

        BATCHES = CHUNKS * VB
        GATHERS = CHUNKS * GB
        RANK = 6
        DEC = 9
        PARTS = 4
        PAIRS = PIECES // 2

        table_v = [t.rearrange("(p i) f -> p i f", p=P) for t in table]
        lookup_v = lookup.rearrange("(p i) f -> p i f", p=P)
        QT = NT // 4

        def scale_lookup(eng, q, step):
            part = acc[:, q * QT:(q + 1) * QT, :]
            done = 2 * q if step is lookup_scaled else 0
            eng.tensor_tensor(part, part, dinv[:, q * QT:(q + 1) * QT].unsqueeze(2).broadcast_to([P, QT, FEAT]),
                              ALU.mult).then_inc(step, 1)
            eng.wait_ge(step, done + 1)
            eng.tensor_tensor(part, part, b2_rep[:, :].unsqueeze(1).broadcast_to([P, QT, FEAT]),
                              ALU.add).then_inc(step, 1)

        def piece_of(i, b):
            return acc[:, bass.ds((i * 2 + b) * PT, PT), :]

        block = ctx.enter_context(nc.Block())

        @block.sync
        def _(sp):
            ei = edge_index.rearrange("a (p c) -> a p c", p=EP)
            sp.dma_start(cols[0:EP, :], ei[1]).then_inc(cols_loaded, 16)
            sp.dma_start(w1_sb[:, :], W1T).then_inc(weights_loaded, 16)
            sp.dma_start(w2_sb[:, :], W2).then_inc(weights_loaded, 16)
            sp.dma_start(b1_sb[:, :], b1.rearrange("(p a) -> p a", a=1)).then_inc(weights_loaded, 16)
            sp.dma_start(b2_rep[:, :], b2.rearrange("(a f) -> a f", a=1).broadcast_to([P, FEAT])).then_inc(weights_loaded, 16)
            for b in range(2):
                sp.dma_start(emb_sb[:, b, :], embT[:, b * BN:(b + 1) * BN]).then_inc(emb_loaded[b], 16)
            sp.dma_start(rows[0:EP, :], ei[0]).then_inc(rows_loaded, 16)
            sp.dma_start(ask_i[:, :], r_input.rearrange("(p t) -> p t", p=P)).then_inc(ask_loaded, 16)
            def write_table(r):
                with sp.Fori(0, PAIRS) as i:
                    for b in range(2):
                        sp.wait_ge(part_lo, i * 2 + (r * PIECES + b + 1))
                        sp.dma_start(table_v[r][:, bass.ds((i * 2 + b) * PT, PT), :],
                                     split[:, b, :, :, :].rearrange("p t c f -> p t (c f)")).then_inc(table_written[b], 16)

            sp.wait_ge(base_step, BASE_STEPS)
            for a in range(2):
                sp.dma_start(visits_dram[a].rearrange("c (p k) -> p c k", p=P),
                             visit_at[:, a, :].rearrange("p (c k) -> p c k", c=CHUNKS)).then_inc(visits_stored, 16)
            sp.wait_ge(visits_stored, 16 * 2)
            sp.dma_start(visits[:, :].rearrange("a (c t) -> a c t", c=CHUNKS), visits_dram[:, :, 0:CV]).then_inc(visits_loaded, 16)
            write_table(0)
            write_table(1)
            for q in range(4):
                if q < 3:
                    sp.wait_ge(lookup_scaled, 2 * (q + 1))
                else:
                    sp.wait_ge(pool_scaled, 2)
                sp.dma_start(lookup_v[:, q * QT:(q + 1) * QT, :], acc[:, q * QT:(q + 1) * QT, :]).then_inc(lookup_written, 16)
            out_v = out.rearrange("(p t) f -> p t f", p=P)
            with sp.Fori(0, OUT_ITERS) as i:
                for h in range(2):
                    sp.wait_ge(rows_fetched[h], i * (16 * W8) + 16 * W8)
                    sp.dma_start(out_v[:, bass.ds(i * (2 * W8) + h * W8, W8), :], out_rows[:, h, :, :]).then_inc(out_written[h], 16)
            for h in range(2):
                sp.wait_ge(out_written[h], 16 * OUT_ITERS)

        @block.gpsimd
        def _(pool):
            pool.iota(ramp8_i[:, :, :], pattern=[[1, 256], [0, W8]], base=0, channel_multiplier=0).then_inc(ints_made, 1)
            pool.memset(zeros_f[:, :], 0.0).then_inc(ints_made, 1)
            pool.memset(ones[:, :], 1.0).then_inc(ints_made, 1)
            pool.memset(one_col[:, :], 1.0).then_inc(ints_made, 1)
            pool.iota(ramp_i[:, :], pattern=[[1, BN]], base=0, channel_multiplier=0).then_inc(ints_made, 1)
            pool.iota(visit_no_i[:, :], pattern=[[1, BT]], base=0, channel_multiplier=BT).then_inc(ints_made, 1)
            pool.wait_ge(ints_made, 6)
            pool.affine_select(out=before[:, :], in_=ones[:, :], compare_op=ALU.is_gt, fill=0.0,
                               base=0, pattern=[[1, P]], channel_multiplier=-1).then_inc(triangles_made, 1)
            pool.affine_select(out=not_before[:, :], in_=ones[:, :], compare_op=ALU.is_ge, fill=0.0,
                               base=0, pattern=[[-1, P]], channel_multiplier=1).then_inc(triangles_made, 1)
            def pool_piece(i, b):
                pool.wait_ge(emb_scaled, i * 7 + (4 + 3 * b + 2))
                if not isinstance(i, int):
                    pool.wait_ge(table_written[b], i * 16)
                pool.sem_inc(waits_passed, 1)
                done = i * (2 * PARTS) + b * PARTS
                pool.tensor_copy(split[:, b, :, 0, :], piece_of(i, b)).then_inc(part_step, 1)
                pool.wait_ge(part_step, done + 1)
                pool.sem_inc(waits_passed, 1)
                pool.tensor_tensor(rest[:, b, :, :], piece_of(i, b), split[:, b, :, 0, :], ALU.subtract).then_inc(part_step, 1)
                pool.wait_ge(part_step, done + 2)
                pool.sem_inc(waits_passed, 1)
                pool.tensor_copy(split[:, b, :, 1, :], rest[:, b, :, :]).then_inc(part_step, 1)
                pool.wait_ge(part_step, done + 3)
                pool.sem_inc(waits_passed, 1)
                pool.tensor_tensor(rest[:, b, :, :], rest[:, b, :, :], split[:, b, :, 1, :], ALU.subtract).then_inc(part_step, 1)
                pool.wait_ge(part_step, done + 4)
                pool.sem_inc(waits_passed, 1)
                pool.tensor_copy(split[:, b, :, 2, :], rest[:, b, :, :]).then_inc(part_lo, 1)

            for b in range(2):
                pool_piece(0, b)
            with pool.Fori(1, PAIRS) as i:
                for b in range(2):
                    pool_piece(i, b)
            for r in range(2):
                if r == 1:
                    with pool.Fori(0, PAIRS) as i:
                        for b in range(2):
                            pool.wait_ge(part_hi, i * 2 + (b + 1))
                            pool.tensor_tensor(rest[:, b, :, :], piece_of(i, b), split[:, b, :, 0, :],
                                               ALU.subtract).then_inc(rest_hi, 1)
                for b in range(2):
                    pool.wait_ge(table_written[b], 16 * PAIRS * (r + 1))
                def gather(place, k):
                    pool.sem_inc(waits_passed, 1)
                    pool.indirect_dma_start(
                        out=place, out_offset=None, in_=table[r],
                        in_offset=bass.IndirectOffsetOnAxis(ap=source8[:, k:k + 1], axis=0)).then_inc(gathered[k], 16)

                if r == 0:
                    with pool.Fori(0, BATCHES) as g:
                        for k in range(W8):
                            if k % 4 == 0:
                                pool.wait_ge(sources_staged, g * 2 + (1 + k // 4))
                            pool.wait_ge(visits_multiplied, g * W8 + (k + 1 + VISIT_CREDIT - W8))
                            gather(gath[:, k, :], k)
                    continue

                def gather_half_ring(c, q, half, freed):
                    for h in range(HALF_RING):
                        for k in range(W8):
                            if k % 4 == 0:
                                pool.wait_ge(sources_staged, c * (2 * GB) + q * (2 * HALF_RING) + (2 * (BATCHES + h) + 1 + k // 4))
                            pool.wait_ge(visits_multiplied, c * CV + q * (HALF_RING * W8) +
                                         ((BATCHES + h + freed) * W8 + k + 1 + VISIT_CREDIT))
                            gather(gath[:, (half * HALF_RING + h) * W8 + k, :], k)

                def gather_chunk(c, odd):
                    for q in range(2):
                        gather_half_ring(c, q, (odd + q) % 2, GB - VB - RINGB + LAG)
                    with pool.Fori(1, GB // RINGB) as i:
                        for q in range(2):
                            gather_half_ring(c, i * 2 + q, (odd + q) % 2, LAG - RINGB)
                    gather_half_ring(c, GB // HALF_RING - 1, odd, LAG - RINGB)

                with pool.Fori(0, CHUNKS // 2) as i:
                    for odd in range(2):
                        gather_chunk(i * 2 + odd, odd)
                gather_chunk(CHUNKS - 1, 0)
            pool.wait_ge(visits_added, 2 * BATCHES * W8 + CREDIT)
            scale_lookup(pool, 3, pool_scaled)
            pool.wait_ge(lookup_written, 16 * 4)

            def fetch_half(i, h):
                pool.wait_ge(asks_staged[h], i + 1)
                if not isinstance(i, int):
                    pool.wait_ge(out_written[h], i * 16)
                pool.sem_inc(waits_passed, 1)
                for k in range(W8):
                    pool.indirect_dma_start(
                        out=out_rows[:, h, k, :], out_offset=None, in_=lookup,
                        in_offset=bass.IndirectOffsetOnAxis(ap=ask8[:, h, k:k + 1], axis=0)).then_inc(rows_fetched[h], 16)

            for h in range(2):
                fetch_half(0, h)
            with pool.Fori(1, OUT_ITERS) as i:
                for h in range(2):
                    fetch_half(i, h)

        @block.scalar
        def _(act):
            act.wait_ge(ints_made, 6)
            act.copy(ramp8[:, :, :], ramp8_i[:, :, :]).then_inc(ramps_cast, 1)
            act.wait_ge(edge_step, 1)
            act.copy(edge_hi[0:EP, :], bits[0:EP, :]).then_inc(edge_cast, 1)
            act.wait_ge(edge_step, 2)
            act.copy(edge_lo[0:EP, :], digit_i[0][0:EP, :]).then_inc(edge_cast, 1)
            act.wait_ge(weights_loaded, 16 * 4)
            act.activation(b1_rep[:, :], ones[:, :], ACT.Copy, scale=b1_sb[:, 0:1]).then_inc(b1_spread, 1)
            act.wait_ge(w12_done, 1)
            act.copy(w12[:, :], w_ps[0:FEAT, 0:FEAT]).then_inc(w12_copied, 1)
            act.copy(c_rep[:, :], w_ps[:, FEAT:2 * FEAT]).then_inc(w12_copied, 1)
            act.wait_ge(edge_step, 3)
            act.copy(edge_blk[0:EP, :], digit_i[1][0:EP, :]).then_inc(edge_cast, 1)
            act.copy(ramp[:, :], ramp_i[:, :]).then_inc(ramps_cast, 1)
            act.copy(visit_no[:, :], visit_no_i[:, :]).then_inc(ramps_cast, 1)
            with act.Fori(0, CHUNKS) as c:
                act.wait_ge(hist_added, c * CB + (CB + 2))
                act.copy(counts[:, bass.ds(c * SLOTS, SLOTS)], count_ps).then_inc(counts_copied, 1)
            act.wait_ge(deg_step, 1)
            act.activation(dtmp[:, :], deg[:, :], ACT.Sqrt).then_inc(root_taken, 1)

            def split_parts():
                with act.Fori(0, PAIRS) as i:
                    for b in range(2):
                        act.wait_ge(scaled, i * 2 + (b + 1))
                        act.wait_ge(table_written[b], i * 16 + 16 * PAIRS)
                        act.copy(split[:, b, :, 0, :], piece_of(i, b)).then_inc(part_hi, 1)
                    for b in range(2):
                        act.wait_ge(rest_hi, i * 2 + (b + 1))
                        act.copy(split[:, b, :, 1, :], rest[:, b, :, :]).then_inc(part_mid, 1)
                    for b in range(2):
                        act.wait_ge(rest_mid, i * 2 + (b + 1))
                        act.copy(split[:, b, :, 2, :], rest[:, b, :, :]).then_inc(part_lo, 1)

            def scale_column(s, j, b):
                act.wait_ge(columns_placed, s * W8 + (j + 1))
                for k in range(2):
                    act.activation(piece[0:EP, k, j, :], prt_onehot[0:EP, b, :, j], ACT.Copy,
                                   scale=digit[k][0:EP, bass.ds(s * W8 + j, 1)]).then_inc(pieces_ready, 1)

            def act_onehot(g, k):
                n = g * len(ON_ACT) + ON_ACT.index(k)
                if k == ON_ACT[0]:
                    act.wait_ge(targets_staged, g + 1)
                act.wait_ge(act_onehots, n + 1)
                act.activation(distance[:, :], ramp[:, :], ACT.Abs, bias=target8[:, k:k + 1], scale=-1.0).then_inc(distances, 1)
                act.wait_ge(distances, n + 1)
                act.wait_ge(visits_multiplied, g * W8 + (k + 1 + VISIT_CREDIT - RING))
                act.activation(target_onehot[:, k % RING, :], distance[:, :], ACT.Relu, bias=one_col[:, 0:1],
                               scale=-1.0).then_inc(act_onehots, 1)

            def stage_sources(g, total, h):
                for k in range(4 * h, 4 * h + 4):
                    act.wait_ge(gathered[k], total * 16)
                act.copy(source8[:, 4 * h:4 * h + 4], source[:, bass.ds(g * W8 + 4 * h, 4)]).then_inc(sources_staged, 1)

            def sort_batch(s, b, load):
                act.wait_ge(rank_step, s * RANK + RANK)
                for j in range(W8):
                    scale_column(s, j, b)
                    if load and j == W8 - 2:
                        act.wait_ge(emb_multiplied, s + 1)
                        act.dma_start(emb_sb[:, b, :], embT[:, bass.ds((s + 2) * BN, BN)]).then_inc(emb_loaded[b], 16)

            with act.Fori(0, (GROUPS - 3) // 2) as i:
                for b in range(2):
                    sort_batch(i * 2 + b, b, True)
            for s in range(GROUPS - 3, CB):
                sort_batch(s, s % 2, s + 2 < GROUPS)
            act.wait_ge(decode_step, DEC)
            for h in range(2):
                act.copy(source8[:, 4 * h:4 * h + 4], source[:, 4 * h:4 * h + 4]).then_inc(sources_staged, 1)

            def visit_batch(g, then):
                for h in range(2):
                    act_onehot(g, ON_ACT[h])
                    if then:
                        stage_sources(g + 1, g + 1, h)

            with act.Fori(1, CHUNKS) as c:
                with act.Fori(0, CB // 2) as i:
                    for b in range(2):
                        s = c * CB + i * 2 + b
                        g = (c - 1) * VB + i * 2 + b
                        act_onehot(g, ON_ACT[0])
                        act.wait_ge(rank_step, s * RANK + RANK)
                        for j in range(W8):
                            scale_column(s, j, b)
                            if j == 1:
                                stage_sources(g + 1, g + 1, 0)
                            if j == 3:
                                act_onehot(g, ON_ACT[1])
                            if j == W8 - 2:
                                stage_sources(g + 1, g + 1, 1)
                act.wait_ge(decode_step, c * DEC + DEC)
                with act.Fori(CB, VB) as i:
                    visit_batch((c - 1) * VB + i, True)
            with act.Fori((CHUNKS - 1) * VB, BATCHES - 1) as g:
                visit_batch(g, True)
            visit_batch(BATCHES - 1, False)
            split_parts()
            place_of = [act.alloc_register(f"place_of_{k}") for k in range(W8)]

            def ring_batch(c, v, tiles, own=True):
                act.load(place_of, visits[1:2, bass.ds((c * VB + v) * W8, W8)])
                g = c * VB + v
                for k in range(W8):
                    if tiles is not None and k % 4 == 0:
                        stage_sources(tiles, tiles + BATCHES, k // 4)
                    if own:
                        act.wait_ge(gathered[k], (c * GB + v) * 16 + (BATCHES + 1) * 16)
                    act.wait_ge(visits_multiplied, g * W8 + (BATCHES * W8 + k + 1 + VISIT_CREDIT - W8))
                    place = act.snap(place_of[k], min_val=0, max_val=RINGT - 1)
                    act.copy(visit_rows[:, k, :], gath[:, bass.ds(place, 1), :].rearrange("p a f -> p (a f)")).then_inc(rows_copied, 1)

            act.wait_ge(visits_loaded, 16)
            act.wait_ge(ask_step, ASK_STEPS)
            act.wait_ge(sources_ready, 2)
            with act.Fori(0, LEAD) as g:
                for h in range(2):
                    stage_sources(g, g + BATCHES, h)

            def chunk_blocks(c):
                with act.Fori(0, HALF_RING - 1) as m:
                    for x in range(HALF_RING + 1):
                        tiles = c * GB + m * HALF_RING + (LEAD + x) if x < HALF_RING else None
                        ring_batch(c, m * (HALF_RING + 1) + x, tiles)

            def last_block(c, last):
                for x in range(HALF_RING):
                    v = (HALF_RING - 1) * (HALF_RING + 1) + x
                    if x == 1 and not last:
                        act.wait_ge(sources_ready, c + 3)
                    ring_batch(c, v, None if last and x > 0 else c * GB + (HALF_RING - 1) * HALF_RING + LEAD + x, own=v < GB)

            with act.Fori(0, CHUNKS - 1) as c:
                chunk_blocks(c)
                last_block(c, False)
            chunk_blocks(CHUNKS - 1)
            last_block(CHUNKS - 1, True)
            act.wait_ge(ask_step, ASK_STEPS)
            for h in range(2):
                act.copy(ask8[:, h, :], ask_i[:, h * W8:(h + 1) * W8]).then_inc(asks_staged[h], 1)
            with act.Fori(1, OUT_ITERS) as i:
                for h in range(2):
                    act.wait_ge(rows_fetched[h], i * (16 * W8))
                    act.copy(ask8[:, h, :], ask_i[:, bass.ds(i * (2 * W8) + h * W8, W8)]).then_inc(asks_staged[h], 1)

        @block.tensor
        def _(pe):
            def clear(bank_ap):
                return pe.matmul(bank_ap, zeros[:, 0:P], zeros[:, 0:bank_ap.shape[1]], start=True, stop=False,
                                 skip_group_check=True)

            def add(dst, lhsT, rhs):
                return pe.matmul(dst, lhsT, rhs, start=False, stop=False, skip_group_check=True)

            pe.sem_inc(visits_multiplied, VISIT_CREDIT)
            pe.sem_inc(columns_placed, CREDIT)
            pe.sem_inc(hist_added, 2)
            pe.sem_inc(degrees_added, 2)
            pe.sem_inc(rank_advanced, 1)
            pe.wait_ge(weights_loaded, 16 * 4)
            pe.wait_ge(b1_spread, 1)
            pe.matmul(w_ps[0:FEAT, 0:FEAT], w1_sb[:, :], w2_sb[:, :], start=True, stop=True)
            pe.matmul(w_ps[:, FEAT:2 * FEAT], b1_rep[:, :], w2_sb[:, :], start=True, stop=True).then_inc(w12_done, 1)
            pe.wait_ge(w12_copied, 2)
            clear(deg_ps)
            pe.wait_ge(triangles_made, 2)
            with pe.Fori(0, CHUNKS) as c:
                pe.wait_ge(counts_copied, c + 1)
                clear(count_ps)
                with pe.Fori(0, CB // 2) as i:
                    for b in range(2):
                        pe.wait_ge(hist_onehots, c * (2 * CB) + i * 4 + (2 * b + 2))
                        for j in range(W8):
                            last = add(deg_ps, lo_onehot[0:EP, b, :, j], hi_onehot[0:EP, b, :, j])
                        last.then_inc(degrees_added, 1)
                        for k in range(BT):
                            last = add(count_ps, ones[0:EP, :],
                                       hi_onehot[0:EP, b, :, :].rearrange("p (n k) j -> p n k j", k=BT)[:, :, k, :])
                        last.then_inc(hist_added, 1)
            clear(rank_ps).then_inc(rank_zeroed, 1)

            def rank_before(s):
                pe.wait_ge(blk_onehots, s + 1)
                add(rank_ps, before[0:EP, :], blk_onehot[0:EP, :, :]).then_inc(rank_summed, 1)

            def rank_rest(s):
                pe.wait_ge(rank_step, s * RANK + 1)
                add(rank_ps, not_before[0:EP, :], blk_onehot[0:EP, :, :]).then_inc(rank_advanced, 1)

            def place_column(s, j):
                pe.wait_ge(pieces_ready, s * (2 * W8) + (2 * j + 2 + PIECE_CREDIT))
                pe.wait_ge(tcol_onehots, s * W8 + (j + 1))
                for k in range(2):
                    last = add(place_ps[k], piece[0:EP, k, j, :], tcol_onehot[0:EP, j % RING, :])
                last.then_inc(columns_placed, 1)

            def multiply_visit(g, k, second):
                if second:
                    pe.wait_ge(target_onehots, g * W8 + (k + 2 - BATCHES * len(ON_ACT)))
                    pe.wait_ge(rows_copied, g * W8 + (k + 1 - BATCHES * W8))
                else:
                    if k in ON_ACT:
                        pe.wait_ge(act_onehots, g * len(ON_ACT) + (ON_ACT.index(k) + 2))
                    else:
                        pe.wait_ge(target_onehots, g * ON_DVE + (dve_rank(k) + 2))
                    pe.wait_ge(gathered[k], g * 16 + 16)
                pe.wait_ge(visits_added, g * W8 + (k + 1 + CREDIT - RING))
                row = visit_rows[:, k, :] if second else gath[:, k, :]
                for n in range(BT):
                    for part in range(3):
                        last = pe.matmul(visit_ps[k % RING][:, n * FEAT:(n + 1) * FEAT],
                                         target_onehot[:, k % RING, n * P:(n + 1) * P],
                                         row[:, part * FEAT:(part + 1) * FEAT],
                                         start=(part == 0), stop=(part == 2))
                last.then_inc(visits_multiplied, 1)

            def plain_batch(g, second=False):
                for k in range(W8):
                    multiply_visit(g, k, second)

            def turn_sources(c):
                pe.wait_ge(sources_spread, c + 1)
                for k in range(BT):
                    last = pe.matmul(turned_ps[:, k * P:(k + 1) * P], visit_source.rearrange("p (i k) -> p k i", k=BT)[:, k, :],
                                     identity[:, :], start=True, stop=True)
                last.then_inc(turned_made, 1)
                pe.wait_ge(turned_copied, c + 1)
                pe.wait_ge(visit_tiles, c * BT + BT)
                pe.wait_ge(sources_ready, c + 1)
                for k in range(BT):
                    last = pe.matmul(tiles_ps, turned[0:CV // BT, k * P:(k + 1) * P], visit_tile[0:CV // BT, k, :],
                                     start=(k == 0), stop=(k == BT - 1))
                last.then_inc(tiles_made, 1)

            def open_chunk(c):
                if not isinstance(c, int):
                    pe.wait_ge(decode_step, c * DEC)
                pe.wait_ge(rank_seeded, c + 1)
                for k in range(2):
                    clear(place_ps[k])

            open_chunk(0)
            rank_before(0)
            rank_rest(0)

            def sort_batch(i, b):
                s = i * 2 + b
                rank_before(s + 1)
                place_column(s, 0)
                rank_rest(s + 1)
                place_column(s, 1)
                pe.wait_ge(emb_loaded[b], i * 16 + 16)
                pe.wait_ge(emb_scaled, s + 1)
                for k in range(BT):
                    last = pe.matmul(emb_ps[b][:, k * FEAT:(k + 1) * FEAT], emb_sb[:, b, k * P:(k + 1) * P], w12[:, :],
                                     start=True, stop=True)
                last.then_inc(emb_multiplied, 1)
                for j in range(2, W8):
                    place_column(s, j)

            with pe.Fori(0, CB // 2 - 1) as i:
                for b in range(2):
                    sort_batch(i, b)
            sort_batch(CB // 2 - 1, 0)
            for j in range(W8):
                place_column(CB - 1, j)
            with pe.Fori(1, CHUNKS) as c:
                open_chunk(c)
                rank_before(c * CB)
                rank_rest(c * CB)

                def both(at, more):
                    s, g = c * CB + at, (c - 1) * VB + at
                    if more:
                        rank_before(s + 1)
                    for k in range(W8):
                        multiply_visit(g, k, False)
                        place_column(s, k)
                        if more and k == 0:
                            rank_rest(s + 1)

                with pe.Fori(0, CB // 2 - 1) as i:
                    for b in range(2):
                        both(i * 2 + b, True)
                both(CB - 2, True)
                both(CB - 1, False)
                with pe.Fori(CB, VB) as i:
                    plain_batch((c - 1) * VB + i)
            pe.wait_ge(identity_made, 1)
            turn_sources(0)
            with pe.Fori((CHUNKS - 1) * VB, BATCHES) as g:
                plain_batch(g)
            with pe.Fori(0, CHUNKS - 1) as c:
                with pe.Fori(0, GB // 2) as i:
                    plain_batch(c * VB + i + BATCHES, second=True)
                turn_sources(c + 1)
                with pe.Fori(GB // 2, VB) as i:
                    plain_batch(c * VB + i + BATCHES, second=True)
            with pe.Fori(2 * BATCHES - VB, 2 * BATCHES) as g:
                plain_batch(g, second=True)

        @block.vector
        def _(dve):
            dve.sem_inc(emb_scaled, 2)
            dve.sem_inc(counts_copied, 1)
            dve.sem_inc(pieces_ready, PIECE_CREDIT)
            dve.sem_inc(target_onehots, 1)
            dve.sem_inc(act_onehots, 1)
            dve.sem_inc(visits_added, CREDIT)
            dve.sem_inc(sources_ready, 1)

            def chain(step, first=0):
                n = [first]

                def link(ins):
                    n[0] += 1
                    ins.then_inc(step, 1)
                    dve.wait_ge(step, n[0])
                return link

            E = slice(0, EP)
            step = chain(edge_step)
            dve.wait_ge(cols_loaded, 16)
            step(dve.tensor_scalar(bits[E, :], cols[E, :], 7, None, ALU.logical_shift_right))
            step(dve.tensor_scalar(digit_i[0][E, :], cols[E, :], P - 1, None, ALU.bitwise_and))
            step(dve.tensor_scalar(digit_i[1][E, :], cols[E, :], 9, None, ALU.logical_shift_right))
            step(dve.tensor_scalar(cols[E, :], cols[E, :], BN - 1, None, ALU.bitwise_and))
            dve.wait_ge(rows_loaded, 16)
            dve.wait_ge(edge_cast, 1)
            step(dve.tensor_scalar(bits[E, :], rows[E, :], 7, None, ALU.logical_shift_right))
            step(dve.tensor_scalar(rows[E, :], rows[E, :], P - 1, None, ALU.bitwise_and))
            step(dve.scalar_tensor_tensor(rows[E, :], rows[E, :], float(NT), bits[E, :], ALU.mult, ALU.add))
            step(dve.tensor_scalar(bits[E, :], rows[E, :], 3, None, ALU.logical_shift_right))
            step(dve.tensor_scalar(rows[E, :], rows[E, :], 7, None, ALU.bitwise_and))
            dve.wait_ge(edge_cast, 3)
            step(dve.tensor_scalar(digit[0][E, :], bits[E, :], float(HALF), -float(CODE + 1), ALU.is_ge, ALU.mult))
            step(dve.scalar_tensor_tensor(digit[0][E, :], bits[E, :], 1.0, digit[0][E, :], ALU.add, ALU.add))
            step(dve.scalar_tensor_tensor(digit[1][E, :], rows[E, :], float(BN), cols[E, :], ALU.mult, ALU.add))
            step(dve.tensor_scalar(digit[1][E, :], digit[1][E, :], -float(HALF), None, ALU.add))

            dve.wait_ge(ramps_cast, 1)
            with dve.Fori(0, CHUNKS * CB // 2) as i:
                for b in range(2):
                    for dst, src, width, used in ((lo_onehot, edge_lo, P, degrees_added), (hi_onehot, edge_hi, NT, hist_added)):
                        dve.wait_ge(used, i * 2 + (b + 1))
                        dve.tensor_tensor(dst[E, b, :, :], ramp8[E, 0:width, :],
                                          src[E, bass.ds(i * (2 * W8) + b * W8, W8)].unsqueeze(1).broadcast_to([EP, width, W8]),
                                          ALU.is_equal).then_inc(hist_onehots, 1)

            step = chain(deg_step)
            dve.wait_ge(hist_added, CHUNKS * CB + 2)
            step(dve.tensor_scalar(deg[:, :], deg_ps, 1.0, 1.0, ALU.add, ALU.max))
            dve.wait_ge(root_taken, 1)
            step(dve.reciprocal(dinv[:, :], dtmp[:, :]))
            step(dve.tensor_tensor(dtmp[:, :], dinv[:, :], dinv[:, :], ALU.mult))
            step(dve.tensor_tensor(dtmp[:, :], dtmp[:, :], deg[:, :], ALU.mult))
            step(dve.tensor_scalar(dtmp[:, :], dtmp[:, :], -0.5, 1.5, ALU.mult, ALU.add))
            step(dve.tensor_tensor(dinv[:, :], dinv[:, :], dtmp[:, :], ALU.mult))

            def scale_piece(i, b):
                part = piece_of(i, b)
                by = dinv[:, bass.ds((i * 2 + b) * PT, PT)].unsqueeze(2).broadcast_to([P, PT, FEAT])
                n = i * 4 + 2 * b
                dve.tensor_tensor(part, part, by, ALU.mult).then_inc(scale_step, 1)
                dve.wait_ge(scale_step, n + 1)
                dve.tensor_tensor(part, part, c_rep[:, :].unsqueeze(1).broadcast_to([P, PT, FEAT]),
                                  ALU.add).then_inc(scale_step, 1)
                dve.wait_ge(scale_step, n + 2)
                dve.tensor_tensor(part, part, by, ALU.mult).then_inc(scaled, 1)

            def rest_piece(i, b):
                dve.wait_ge(part_mid, i * 2 + (b + 1))
                dve.tensor_tensor(rest[:, b, :, :], rest[:, b, :, :], split[:, b, :, 1, :],
                                  ALU.subtract).then_inc(rest_mid, 1)

            def make_table():
                for b in range(2):
                    scale_piece(0, b)
                with dve.Fori(1, PAIRS) as i:
                    for b in range(2):
                        scale_piece(i, b)
                    for b in range(2):
                        rest_piece(i - 1, b)
                for b in range(2):
                    rest_piece(PAIRS - 1, b)

            step = chain(base_step)
            dve.wait_ge(counts_copied, CHUNKS + 1)
            dve.wait_ge(ramps_cast, 3)
            per_slot = counts[:, :].rearrange("p (n j) -> p n j", j=W8)
            flat = tot[:, :, :].rearrange("p c n -> p (c n)")
            flat_i = tot_i[:, :, :].rearrange("p c n -> p (c n)")
            step(dve.tensor_reduce(flat, per_slot, AX.X, ALU.add))
            for c in range(CHUNKS):
                step(dve.tensor_tensor_scan(seed[:, c, :], counts[:, c * SLOTS:(c + 1) * SLOTS], zeros_f[:, 0:SLOTS],
                                            0.0, ALU.add, ALU.add))
            seed_flat = seed[:, :, :].rearrange("p c s -> p (c s)")
            seed_slot = seed[:, :, :].rearrange("p c (n j) -> p (c n) j", j=W8)
            low_flat, low_i = (a.rearrange("p c n -> p (c n)") for a in (low_f, low[:, :, :]))
            end_flat = endt[:, :, :].rearrange("p c n -> p (c n)")
            step(dve.tensor_tensor(seed_flat, seed_flat, counts[:, :], ALU.subtract))
            step(dve.tensor_tensor(flat_i, seed_slot[:, :, 0], flat, ALU.add))
            step(dve.tensor_scalar(low_i, flat_i, P - 1, None, ALU.bitwise_and))
            step(dve.tensor_scalar(flat_i, flat_i, 7, None, ALU.logical_shift_right))
            step(dve.tensor_scalar(flat, flat, 0.0, None, ALU.is_gt))
            step(dve.scalar_tensor_tensor(flat, low_i, 0.0, flat, ALU.is_gt, ALU.mult))
            for c in range(CHUNKS):
                step(dve.tensor_tensor_scan(endt[:, c, :], tot[:, c, :], zeros_f[:, 0:NB], 0.0, ALU.add, ALU.add))
            step(dve.tensor_tensor(low_flat, end_flat, flat, ALU.subtract))
            step(dve.scalar_tensor_tensor(seed_slot, low_flat.unsqueeze(2).broadcast_to([P, CHUNKS * NB, W8]), float(P),
                                          seed_slot, ALU.mult, ALU.add))
            step(dve.tensor_tensor(end_flat, end_flat, flat_i, ALU.add))
            visit_shape = [P, CHUNKS, BT, NB]
            step(dve.tensor_tensor(ended[:, :, :, :], endt[:, :, :].unsqueeze(2).broadcast_to(visit_shape),
                                   visit_no[:, :].unsqueeze(1).unsqueeze(3).broadcast_to(visit_shape), ALU.is_le))
            step(dve.tensor_reduce(blk_f[:, :], ended[:, :, :, :].rearrange("p c k n -> p (c k) n"), AX.X, ALU.add))
            step(dve.tensor_scalar(visit_at[:, 0, :], blk_f[:, :], float(NB - 1), None, ALU.min))
            step(dve.tensor_tensor(ended[:, :, :, :], ended[:, :, :, :], tot[:, :, :].unsqueeze(2).broadcast_to(visit_shape),
                                   ALU.mult))
            step(dve.tensor_reduce(blk_f[:, :], ended[:, :, :, 0:NB - 1].rearrange("p c k n -> p (c k) n"), AX.X, ALU.add))
            step(dve.tensor_tensor(tile_of[:, :, :], visit_no[:, :].unsqueeze(1).broadcast_to([P, CHUNKS, BT]),
                                   blk_f[:, :].rearrange("p (c k) -> p c k", k=BT), ALU.subtract))
            tile_flat = tile_of[:, :, :].rearrange("p c k -> p (c k)")
            step(dve.tensor_scalar(tile_flat, tile_flat, float(GT - 1), None, ALU.min))
            ring_flat = tile_of_ring[:, :, :].rearrange("p c k -> p (c k)")
            step(dve.tensor_copy(ring_flat, tile_flat))
            for c in range(1, CHUNKS, 2):
                step(dve.tensor_scalar(tile_of_ring[:, c, :], tile_of_ring[:, c, :], float(RINGT // 2), None, ALU.add))
            step(dve.tensor_scalar(tile_i[:, :], ring_flat, float(RECIPROCAL), None, ALU.mult))
            step(dve.tensor_scalar(tile_i[:, :], tile_i[:, :], 16, None, ALU.logical_shift_right))
            step(dve.scalar_tensor_tensor(visit_at[:, 1, :], tile_i[:, :], -float(RINGT), ring_flat, ALU.mult, ALU.add))
            dve.tensor_scalar(identity[:, :], ramp[:, 0:P], float(BT), visit_no[:, 0:1], ALU.mult,
                              ALU.is_equal).then_inc(identity_made, 1)

            def find_asked():
                step = chain(ask_step)
                dve.wait_ge(ask_loaded, 16)
                step(dve.tensor_scalar(ask_f, ask_i[:, :], 0.0, float(NODES), ALU.is_lt, ALU.mult))
                step(dve.tensor_tensor(ask_f, ask_f, ask_i[:, :], ALU.add))
                step(dve.tensor_scalar(ask_t, ask_f, 0.0, float(NODES - 1), ALU.max, ALU.min))
                step(dve.tensor_scalar(ask_i[:, :], ask_t, 7, None, ALU.logical_shift_right))
                step(dve.tensor_scalar(ask_t, ask_t, P - 1, None, ALU.bitwise_and))
                step(dve.scalar_tensor_tensor(ask_i[:, :], ask_t, float(NT), ask_i[:, :], ALU.mult, ALU.add))

            block_of = [dve.alloc_register(f"block_of_{k}") for k in range(W8)]

            def seed_ranks(c):
                dve.wait_ge(rank_advanced, c * CB + 1)
                dve.tensor_copy(rank_ps, seed_flat[:, bass.ds(c * SLOTS, SLOTS)]).then_inc(rank_seeded, 1)

            def block_onehots(s):
                dve.wait_ge(rank_advanced, s + 1)
                dve.tensor_tensor(blk_onehot[E, :, :], ramp8[E, 0:NB, :],
                                  edge_blk[E, bass.ds(s * W8, W8)].unsqueeze(1).broadcast_to([EP, NB, W8]),
                                  ALU.is_equal).then_inc(blk_onehots, 1)

            def pick_ranks(s):
                dve.wait_ge(rank_summed, s + 1)
                dve.tensor_tensor(picked[E, :, :], rank_ps[E, :].rearrange("p (n j) -> p n j", j=W8),
                                  blk_onehot[E, :, :], ALU.mult).then_inc(rank_step, 1)

            def sum_ranks(s):
                dve.wait_ge(rank_step, s * RANK + 1)
                with nc.allow_low_precision(reason="one whole number among zeros"):
                    dve.tensor_reduce(place_i[E, 0, :], picked[E, :, :].rearrange("p n j -> p j n"), AX.X,
                                      ALU.add).then_inc(rank_step, 1)

            def cut_places(s, b):
                dve.wait_ge(rank_step, s * RANK + 2)
                dve.tensor_scalar(place_i[E, 1, :], place_i[E, 0, :], P - 1, None, ALU.bitwise_and).then_inc(rank_step, 1)
                dve.tensor_scalar(tcol[E, b, :], place_i[E, 0, :], 7, None, ALU.logical_shift_right).then_inc(rank_step, 1)

            def cast_places(s):
                dve.wait_ge(rank_step, s * RANK + 3)
                dve.tensor_copy(prt16[E, :], place_i[E, 1, :]).then_inc(rank_step, 1)

            def partition_onehots(s, b):
                dve.wait_ge(rank_step, s * RANK + 5)
                dve.wait_ge(pieces_ready, s * (2 * W8) + (PIECE_CREDIT - 2 * W8))
                dve.tensor_tensor(prt_onehot[E, b, :, :], ramp8[E, 0:P, :],
                                  prt16[E, :].unsqueeze(1).broadcast_to([EP, P, W8]), ALU.is_equal).then_inc(rank_step, 1)

            def column_onehot(s, j, b):
                dve.wait_ge(columns_placed, s * W8 + (j + 1 + CREDIT - RING))
                dve.tensor_scalar(tcol_onehot[E, j % RING, :], ramp[E, 0:CV], tcol[E, b, j:j + 1], None,
                                  ALU.is_equal).then_inc(tcol_onehots, 1)

            def stage_targets(g, total, shared):
                if shared:
                    dve.wait_ge(target_onehots, total * ON_DVE + 1)
                    dve.wait_ge(act_onehots, total * len(ON_ACT) + 1)
                else:
                    dve.wait_ge(target_onehots, total * W8 + (1 - BATCHES * len(ON_ACT)))
                dve.tensor_copy(target8[:, :], target[:, bass.ds(g * W8, W8)]).then_inc(targets_staged, 1)

            def load_blocks(g):
                dve.load(block_of, visits[0:1, bass.ds(g * W8, W8)])

            def target_onehot_of(g, k, shared):
                if shared and k in ON_ACT:
                    return
                if k == 0:
                    dve.wait_ge(targets_staged, g + 1)
                dve.wait_ge(visits_multiplied, g * W8 + (k + 1 + VISIT_CREDIT - RING))
                dve.tensor_scalar(target_onehot[:, k % RING, :], ramp[:, :], target8[:, k:k + 1], None,
                                  ALU.is_equal).then_inc(target_onehots, 1)

            def add_visit(g, k):
                dve.wait_ge(visits_multiplied, g * W8 + (k + 1 + VISIT_CREDIT))
                dve.wait_ge(visits_added, g * W8 + (k + CREDIT))
                blk = dve.snap(block_of[k], min_val=0, max_val=NB - 1)
                dst = acc[:, bass.ds(blk * BT, BT), :]
                dve.tensor_tensor(dst, dst, visit_ps[k % RING].rearrange("p (n f) -> p n f", f=FEAT),
                                  ALU.add).then_inc(visits_added, 1)

            def visit_batch(r, g, shared, then, decoded=None):
                total = g + r * BATCHES
                for k in range(3):
                    target_onehot_of(total, k, shared)
                load_blocks(g)
                add_visit(total, 0)
                for k in range(3, W8):
                    target_onehot_of(total, k, shared)
                    add_visit(total, k - 2)
                add_visit(total, W8 - 2)
                if decoded is not None:
                    dve.wait_ge(decode_step, decoded * DEC + DEC)
                if then is not None:
                    stage_targets(then, total + 1, shared)
                add_visit(total, W8 - 1)

            def decode(c):
                dve.wait_ge(columns_placed, c * (CB * W8) + (CB * W8 + CREDIT))
                n = [0]

                def link(ins):
                    n[0] += 1
                    ins.then_inc(decode_step, 1)
                    if n[0] < DEC:
                        dve.wait_ge(decode_step, c * DEC + n[0])
                link(dve.tensor_scalar(dec[0][:, :], place_ps[0], 0.0, float(CODE + 1), ALU.is_lt, ALU.mult))
                link(dve.tensor_tensor(dec[0][:, :], dec[0][:, :], place_ps[0], ALU.add))
                link(dve.tensor_scalar(dec_i[0][:, :], place_ps[1], float(HALF), None, ALU.add))
                link(dve.tensor_scalar(dec_i[1][:, :], dec_i[0][:, :], 9, None, ALU.logical_shift_right))
                link(dve.scalar_tensor_tensor(dec[1][:, :], dec[0][:, :], float(CODE // BN), dec_i[1][:, :], ALU.mult, ALU.add))
                link(dve.tensor_scalar(dec_i[0][:, :], dec_i[0][:, :], BN - 1, None, ALU.bitwise_and))
                link(dve.tensor_scalar(source[:, bass.ds(c * CV, CV)], dec[1][:, :], -float(CODE // BN), 0.0, ALU.add, ALU.max))
                link(dve.tensor_scalar(dec[1][:, :], dec[0][:, :], 0.0, NOWHERE, ALU.is_equal, ALU.mult))
                link(dve.tensor_tensor(target[:, bass.ds(c * CV, CV)], dec[1][:, :], dec_i[0][:, :], ALU.add))

            def turn_sources(c):
                dve.tensor_copy(visit_source, source[:, bass.ds(c * CV, CV)]).then_inc(sources_spread, 1)
                for k in range(BT):
                    dve.tensor_scalar(visit_tile[0:CV // BT, k, :], ramp[0:CV // BT, 0:GT], tile_of_flat[0:CV // BT, bass.ds(c * BT + k, 1)],
                                      None, ALU.is_equal).then_inc(visit_tiles, 1)
                dve.wait_ge(turned_made, c + 1)
                dve.tensor_copy(turned[0:CV // BT, :], turned_ps).then_inc(turned_copied, 1)
                dve.wait_ge(tiles_made, c + 1)
                dve.wait_ge(sources_spread, c + 1)
                dve.tensor_copy(source[:, bass.ds(c * GT, GT)], tiles_ps).then_inc(sources_ready, 1)

            tile_of_flat = tile_of[:, :, :].rearrange("p c k -> p (c k)")
            dve.wait_ge(rank_zeroed, 1)
            dve.wait_ge(ramps_cast, 3)
            seed_ranks(0)
            def first_places(s):
                block_onehots(s)
                pick_ranks(s)
                sum_ranks(s)
                cut_places(s, 0)
                cast_places(s)
                partition_onehots(s, 0)

            first_places(0)

            def sort_batch(i, b):
                s = i * 2 + b
                block_onehots(s + 1)
                column_onehot(s, 0, b)
                pick_ranks(s + 1)
                column_onehot(s, 1, b)
                sum_ranks(s + 1)
                column_onehot(s, 2, b)
                cut_places(s + 1, 1 - b)
                column_onehot(s, 3, b)
                cast_places(s + 1)
                dve.wait_ge(emb_multiplied, s + 1)
                dve.tensor_tensor(acc[:, bass.ds(s * BT, BT), :], emb_ps[b].rearrange("p (t f) -> p t f", f=FEAT),
                                  dinv[:, bass.ds(s * BT, BT)].unsqueeze(2).broadcast_to([P, BT, FEAT]),
                                  ALU.mult).then_inc(emb_scaled, 1)
                partition_onehots(s + 1, 1 - b)
                for j in range(4, W8):
                    column_onehot(s, j, b)

            with dve.Fori(0, CB // 2 - 1) as i:
                for b in range(2):
                    sort_batch(i, b)
            sort_batch(CB // 2 - 1, 0)
            for j in range(W8):
                column_onehot(CB - 1, j, 1)
            decode(0)
            dve.wait_ge(visits_loaded, 16)
            dve.wait_ge(decode_step, DEC)
            dve.tensor_copy(target8[:, :], target[:, 0:W8]).then_inc(targets_staged, 1)
            with dve.Fori(1, CHUNKS) as c:
                seed_ranks(c)
                first_places(c * CB)

                def both(at, b, first=False, last=False):
                    s, g = c * CB + at, (c - 1) * VB + at
                    for step in BOTH:
                        what, k = step[0], step[-1]
                        if what == "late add":
                            if not first:
                                add_visit(g - 1, k)
                        elif what == "stage":
                            stage_targets(g + 1, g + 1, True)
                        elif what == "column":
                            column_onehot(s, k, b)
                        elif what == "target":
                            target_onehot_of(g, k, True)
                        elif what == "add":
                            add_visit(g, k)
                        elif what == "load":
                            load_blocks(g)
                        elif last:
                            continue
                        elif what == "blocks":
                            block_onehots(s + 1)
                        elif what == "pick":
                            pick_ranks(s + 1)
                        elif what == "sum":
                            sum_ranks(s + 1)
                        elif what == "cut":
                            cut_places(s + 1, 1 - b)
                        elif what == "cast":
                            cast_places(s + 1)
                        elif what == "partitions":
                            partition_onehots(s + 1, 1 - b)

                both(0, 0, first=True)
                with dve.Fori(0, CB // 2 - 1) as i:
                    for b in range(2):
                        both(i * 2 + (1 + b), 1 - b)
                both(CB - 1, 1, last=True)
                for k in LATE:
                    add_visit((c - 1) * VB + (CB - 1), k)
                decode(c)
                with dve.Fori(CB, VB) as i:
                    visit_batch(0, (c - 1) * VB + i, True, (c - 1) * VB + i + 1, decoded=c)
            turn_sources(0)
            with dve.Fori((CHUNKS - 1) * VB, BATCHES - 1) as g:
                visit_batch(0, g, True, g + 1)
            visit_batch(0, BATCHES - 1, True, 0)
            dve.wait_ge(visits_added, BATCHES * W8 + CREDIT)
            make_table()
            find_asked()
            with dve.Fori(0, CHUNKS - 1) as c:
                with dve.Fori(0, GB // 2) as i:
                    visit_batch(1, c * VB + i, False, c * VB + i + 1)
                turn_sources(c + 1)
                with dve.Fori(GB // 2, VB) as i:
                    visit_batch(1, c * VB + i, False, c * VB + i + 1)
            with dve.Fori((CHUNKS - 1) * VB, BATCHES - 1) as g:
                visit_batch(1, g, False, g + 1)
            visit_batch(1, BATCHES - 1, False, None)
            dve.wait_ge(visits_added, 2 * BATCHES * W8 + CREDIT)
            for q in range(3):
                scale_lookup(dve, q, lookup_scaled)


BOTH = [("blocks",), ("target", 0), ("column", 0), ("late add", 6), ("target", 1), ("pick",), ("late add", 7),
        ("load",), ("column", 1), ("sum",), ("target", 2), ("column", 2), ("add", 0), ("cut",), ("column", 3), ("add", 1),
        ("cast",), ("target", 4), ("column", 4), ("add", 2), ("partitions",), ("target", 5), ("column", 5), ("add", 3),
        ("column", 6), ("target", 7), ("add", 4), ("stage",), ("column", 7), ("add", 5)]
LATE = [step[-1] for step in BOTH if step[0] == "late add"]
PIECE_CREDIT = 2 * 2 * W8
BASE_STEPS = 1 + CHUNKS + 6 + CHUNKS + 3 + 3 + 4 + 1 + CHUNKS // 2 + 3
ASK_STEPS = 6


def kernel(**inputs):
    import numpy as np
    import concourse.bacc as bacc
    from concourse.bass_utils import run_bass_kernel_spmd

    emb = np.asarray(inputs["L0_rec_emb"])
    embT = np.zeros((FEAT, NT * P), emb.dtype)
    embT[:, 0:NODES] = emb.T
    arrays = {
        "r_input": np.ascontiguousarray(np.asarray(inputs["r_input"]).reshape(-1)),
        "edge_index": np.ascontiguousarray(inputs["L0_rec_edge_index"]),
        "embT": embT,
        "W1T": np.ascontiguousarray(np.asarray(inputs["L0_rec_W1"]).T),
        "b1": np.ascontiguousarray(inputs["L0_rec_b1"]),
        "W2": np.ascontiguousarray(inputs["L0_rec_W2"]),
        "b2": np.ascontiguousarray(inputs["L0_rec_b2"]),
    }
    nc = bacc.Bacc("TRN2", target_bir_lowering=False, num_devices=1)
    args = [nc.dram_tensor(name, a.shape, mybir.dt.from_np(a.dtype), kind="ExternalInput").ap() for name, a in arrays.items()]
    args.append(nc.dram_tensor("out", [LOOKUPS, FEAT], F32, kind="ExternalOutput").ap())
    build(nc, *args)
    r = run_bass_kernel_spmd(nc, [arrays], core_ids=[0])
    return r.results[0]["out"].reshape(512, 200, FEAT)
```
